# Optimizing a Trainium2 kernel written in Bass

```python
import numpy as np
import jax
import jax.numpy as jnp

def _softmax(x, axis=-1):
    return jax.nn.softmax(x, axis=axis)

def _gelu(x):
    return jax.nn.gelu(x, approximate=True)

def _silu(x):
    return jax.nn.silu(x)

def _sigmoid(x):
    return jax.nn.sigmoid(x)

def _layernorm(x, axis=-1, eps=1e-05):
    m = jnp.mean(x, axis=axis, keepdims=True)
    v = jnp.var(x, axis=axis, keepdims=True)
    return (x - m) / jnp.sqrt(v + eps)

def _scatter_add(tgt, idx, src, axis=0):
    return tgt.at[idx].add(src)

def _segment_sum(src, seg, n):
    return jax.ops.segment_sum(src, seg, n)
kernel_name = 'mk_adj_preln_d2_adj_r2_39f15f'

def setup_inputs(seed: int=0):
    np.random.seed(seed)
    _w = jnp.asarray

    def _rec_inputs():
        import jax
        import jax.numpy as jnp
        _gk = jax.random.key(seed)
        x = -0.0003929 + 0.9999 * jax.random.normal(jax.random.fold_in(_gk, 1), (32, 256, 512), jnp.float32)
        _w = (1.0 + jnp.arange(256, dtype=jnp.float32)) ** (-0.5)
        _w = _w / _w.mean()
        _pij = jnp.clip(0.015625 * _w[:, None] * _w[None, :], 0.0, 1.0)
        _a = jax.random.uniform(jax.random.fold_in(_gk, 2), (256, 256)) < _pij
        _a = jnp.logical_or(_a, jnp.swapaxes(_a, -1, -2))
        _a = jnp.logical_or(_a, jnp.eye(256, dtype=bool))
        _af = _a.astype(jnp.float32)
        _af = _af * jax.random.uniform(jax.random.fold_in(_gk, 3), (256, 256), jnp.float32, 0.05, 0.198159)
        adj = _af
        return (x, adj)
    x, adj = _rec_inputs()

    def _L0_gnn_setup():
        import jax, jax.numpy as jnp
        import numpy as np
        NEG_SLOPE = 0.01
        key = jax.random.key(seed)
        k1, k2, k3, k4, k5 = jax.random.split(key, 5)
        B, C, N, O = (32, 256, 512, 256)
        x = jax.random.normal(k1, (B, C, N), dtype=jnp.float32)
        wq = jax.random.normal(k2, (C,), dtype=jnp.float32) * (1.0 / np.sqrt(C))
        wk = jax.random.normal(k3, (C,), dtype=jnp.float32) * (1.0 / np.sqrt(C))
        wm = jax.random.normal(k4, (O, C), dtype=jnp.float32) * (1.0 / np.sqrt(C))
        bm = jax.random.normal(k5, (O,), dtype=jnp.float32) * 0.01
        return {'x': x, 'wq': wq, 'wk': wk, 'wm': wm, 'bm': bm}
    _L0_gnn_all = _L0_gnn_setup()
    _L0_gnn_in = {k: v for k, v in _L0_gnn_all.items() if k in ('wq', 'wk', 'bm')}
    del _L0_gnn_all

    def _L1_gnn_setup():
        import jax, jax.numpy as jnp
        import numpy as np
        EPS = 1e-08

        def _row_stochastic_causal(A, causal_mask):
            A = A * causal_mask
            deg = jnp.maximum(A.sum(axis=-1, keepdims=True), EPS)
            return A / deg
        key = jax.random.key(seed)
        k = jax.random.split(key, 5)
        B, N, D = (4, 1024, 512)
        s = 1.0 / np.sqrt(D)
        h = jax.random.normal(k[0], (B, N, D), dtype=jnp.float32)
        W_lang = jax.random.normal(k[1], (D, D), dtype=jnp.float32) * s
        W_grav = jax.random.normal(k[2], (D, D), dtype=jnp.float32) * s
        W_V = jax.random.normal(k[3], (D, D), dtype=jnp.float32) * s
        W_O = jax.random.normal(k[4], (D, D), dtype=jnp.float32) * s
        causal_mask = jnp.tril(jnp.ones((N, N), dtype=jnp.float32))
        gate_logit = jnp.zeros((), jnp.float32)
        log_sigma = jnp.zeros((), jnp.float32)
        return {'h': h, 'causal_mask': causal_mask, 'W_lang': W_lang, 'W_grav': W_grav, 'W_V': W_V, 'W_O': W_O, 'gate_logit': gate_logit, 'log_sigma': log_sigma}
    _L1_gnn_all = _L1_gnn_setup()
    _L1_gnn_in = {k: v for k, v in _L1_gnn_all.items() if k in ('W_lang', 'W_grav', 'W_V', 'W_O', 'gate_logit', 'log_sigma')}
    del _L1_gnn_all
    return {'x': x, 'adj': adj, 'L0_gnn_wq': _L0_gnn_in['wq'], 'L0_gnn_wk': _L0_gnn_in['wk'], 'L0_gnn_bm': _L0_gnn_in['bm'], 'L1_gnn_W_lang': _L1_gnn_in['W_lang'], 'L1_gnn_W_grav': _L1_gnn_in['W_grav'], 'L1_gnn_W_V': _L1_gnn_in['W_V'], 'L1_gnn_W_O': _L1_gnn_in['W_O'], 'L1_gnn_gate_logit': _L1_gnn_in['gate_logit'], 'L1_gnn_log_sigma': _L1_gnn_in['log_sigma']}

def reference(x, adj, L0_gnn_wq, L0_gnn_wk, L0_gnn_bm, L1_gnn_W_lang, L1_gnn_W_grav, L1_gnn_W_V, L1_gnn_W_O, L1_gnn_gate_logit, L1_gnn_log_sigma):
    import jax
    import jax.numpy as jnp

    def _L0_gnn_ref(x, wq, wk, wm, bm):
        import jax, jax.numpy as jnp
        import numpy as np
        NEG_SLOPE = 0.01
        q = jnp.einsum('c,bcn->bn', wq, x)
        k = jnp.einsum('c,bcn->bn', wk, x)
        scores = q[:, None, :] + k[:, :, None]
        scores = jnp.where(scores > 0, scores, NEG_SLOPE * scores)
        att = jax.nn.softmax(scores, axis=-1)
        agg = jnp.einsum('bcn,bmn->bcm', x, att)
        out = jnp.einsum('oc,bcm->bom', wm, agg) + bm[None, :, None]
        return jax.nn.relu(out)

    def _L1_gnn_ref(h, causal_mask, W_lang, W_grav, W_V, W_O, gate_logit, log_sigma):
        import jax, jax.numpy as jnp
        import numpy as np
        EPS = 1e-08

        def _row_stochastic_causal(A, causal_mask):
            A = A * causal_mask
            deg = jnp.maximum(A.sum(axis=-1, keepdims=True), EPS)
            return A / deg
        z_l = jnp.einsum('bnd,ed->bne', h, W_lang)
        z_g = jnp.einsum('bnd,ed->bne', h, W_grav)
        v = jnp.einsum('bnd,ed->bne', h, W_V)
        N = h.shape[-2]
        not_eye = 1.0 - jnp.eye(N, dtype=h.dtype)
        zn = z_l / jnp.maximum(jnp.linalg.norm(z_l, axis=-1, keepdims=True), EPS)
        A_l = jnp.maximum(jnp.einsum('bnd,bmd->bnm', zn, zn), 0.0) * not_eye
        sq = jnp.sum(z_g * z_g, axis=-1, keepdims=True)
        d2 = jnp.maximum(sq + jnp.swapaxes(sq, -1, -2) - 2.0 * jnp.einsum('bnd,bmd->bnm', z_g, z_g), 0.0)
        sigma = jnp.exp(log_sigma)
        A_g = jnp.exp(-d2 / (2.0 * sigma * sigma)) * not_eye
        K_l = _row_stochastic_causal(A_l, causal_mask)
        K_g = _row_stochastic_causal(A_g, causal_mask)
        w_l = jax.nn.sigmoid(gate_logit)
        K = w_l * K_l + (1.0 - w_l) * K_g
        out = jnp.einsum('bnm,bmd->bnd', K, v)
        return jnp.einsum('bnd,ed->bne', out, W_O)
    h = jnp.maximum(_layernorm(x, axis=-1), 0.0)
    x = x + _L0_gnn_ref(h, L0_gnn_wq, L0_gnn_wk, adj, L0_gnn_bm)
    h = jnp.maximum(_layernorm(x, axis=-1), 0.0)
    x = x + _L1_gnn_ref(h, adj, L1_gnn_W_lang, L1_gnn_W_grav, L1_gnn_W_V, L1_gnn_W_O, L1_gnn_gate_logit, L1_gnn_log_sigma)
    return x

_drawn_inputs = setup_inputs


def setup_inputs(seed=0):
    import zlib

    import numpy as np

    out = dict(_drawn_inputs(seed))
    spreads = {}
    factors = {'L0_gnn_wq': 8.0, 'L0_gnn_wk': 8.0, 'L0_gnn_bm': 6.807, 'L1_gnn_W_lang': 5.348}
    for name, (base, spread) in spreads.items():
        noise = np.random.default_rng([zlib.crc32(name.encode()), seed]).standard_normal(out[name].shape)
        drawn = base * np.exp(spread * noise) if base else spread * noise
        out[name] = jnp.asarray(drawn.astype(out[name].dtype))
    for name, factor in factors.items():
        out[name] = (out[name] * factor).astype(out[name].dtype)
    return out
```

```python
import concourse.bass as bass
from concourse import mybir
from contextlib import ExitStack


def adjacency_two_layer_kernel(nc: bass.Bass, x, adj, adj_ext, bm, w_lang_t, w_grav_t, w_v, w_o_t,
                               gate_logit, log_sigma, out):
    fp32, fp32r = mybir.dt.float32, mybir.dt.float32r
    ALU = mybir.AluOpType
    ACT = mybir.ActivationFunctionType
    AX = mybir.AxisListType

    B, C, N = x.shape
    PAIRS = B // 2
    CB, NB = C // 128, N // 128
    LN_EPS, TINY = 1e-5, 1e-8
    SLOPE = 0.01
    CE = C + 2

    with ExitStack() as ctx:
        def sb(name, shape, dt=fp32):
            return ctx.enter_context(nc.sbuf_tensor(name, shape, dt))

        def sem(name):
            return ctx.enter_context(nc.semaphore(name))

        wl_hi, wl_lo = sb("wl_hi", [128, NB, N], fp32r), sb("wl_lo", [128, NB, N], fp32r)
        wg_hi, wg_lo = sb("wg_hi", [128, NB, N], fp32r), sb("wg_lo", [128, NB, N], fp32r)
        wov_hi, wov_lo = sb("wov_hi", [128, NB, N], fp32r), sb("wov_lo", [128, NB, N], fp32r)
        ae_hi, ae_lo = sb("ae_hi", [128, CB, CE], fp32r), sb("ae_lo", [128, CB, CE], fp32r)
        adjz = sb("adjz", [128, CB, C])
        bm_rows = sb("bm_rows", [128, C])
        ident = sb("ident", [128, 128])
        minus_half = sb("minus_half", [128, 2])
        gate = sb("gate", [128, 8])
        sig = sb("sig", [128, 8])
        x_in = sb("x_in", [128, 2, CB, N])
        h = sb("h", [128, CB, N])
        h_hi, h_lo = sb("h_hi", [128, CB, N], fp32r), sb("h_lo", [128, CB, N], fp32r)
        hab = sb("hab", [128, 2, C])
        ha_hi, ha_lo = sb("ha_hi", [128, 2, NB, C], fp32r), sb("ha_lo", [128, 2, NB, C], fp32r)
        v_row = sb("v_row", [128, N])
        p_f = sb("p_f", [128, NB, N])
        p_hi, p_lo = sb("p_hi", [128, NB, N], fp32r), sb("p_lo", [128, NB, N], fp32r)
        p_sum = sb("p_sum", [128, N])
        rz_row = sb("rz_row", [128, N])
        x1 = sb("x1", [128, 2, CB, N])
        keep = sb("keep", [128, 2, CB, N])
        h2 = sb("h2", [128, 2, CB, N])
        ht_hi, ht_lo = sb("ht_hi", [128, NB, 2 * C], fp32r), sb("ht_lo", [128, NB, 2 * C], fp32r)
        z_hi, z_lo = sb("z_hi", [128, NB, 2 * C], fp32r), sb("z_lo", [128, NB, 2 * C], fp32r)
        v_hi, v_lo = sb("v_hi", [128, 2 * CB, N], fp32r), sb("v_lo", [128, 2 * CB, N], fp32r)
        g_l = sb("g_l", [128, 2, CB, C])
        g_g = sb("g_g", [128, 2, CB, C])
        rows = sb("rows", [128, 2, 2, C])
        k_f = sb("k_f", [128, 2, CB, C])
        kt_hi, kt_lo = sb("kt_hi", [128, 2, CB, C], fp32r), sb("kt_lo", [128, 2, CB, C], fp32r)
        bn = sb("bn", [128, 4, CB, 6])
        mv = sb("mv", [128, 4, 5, CB])
        var = sb("var", [128, 4, CB])
        nmean = sb("nmean", [128, 4, CB])
        rstd = sb("rstd", [128, 4, CB])
        nmr = sb("nmr", [128, 4, CB])
        qk = sb("qk", [128, 2, NB, 2])
        q_top = sb("q_top", [128, 2])
        q_max = sb("q_max", [128, 2])
        q_less = sb("q_less", [128, 2, NB])
        k_pos = sb("k_pos", [128, 2, NB])
        col_a, col_b, col_v = sb("col_a", [128, 2, NB]), sb("col_b", [128, 2, NB]), sb("col_v", [128, 2, NB])
        z_sum, z_inv = sb("z_sum", [128, 2, NB]), sb("z_inv", [128, 2, NB])
        junk = sb("junk", [128, 128])
        sq_l, sq_g = sb("sq_l", [128, 2, CB]), sb("sq_g", [128, 2, CB])
        sq_lm = sb("sq_lm", [128, 2, CB])
        r_norm = sb("r_norm", [128, 2, CB])
        c_sq = sb("c_sq", [128, 2, CB])
        deg = sb("deg", [128, 2, 2, CB])
        deg2 = sb("deg2", [128, 2, 2, CB])
        deg3 = sb("deg3", [128, 2, 2, CB])
        deg_inv = sb("deg_inv", [128, 2, 2, CB])
        coef = sb("coef", [128, 2, 2, CB])

        bank = [ctx.enter_context(nc.psum_tensor(f"bank{j}", [128, 512], fp32)) for j in range(8)]
        ae_f = h2[:, 0, :, 0:CE]
        L0_BANK, SUM_BANK, L1_BANK = bank[0:2], bank[2:4], bank[4:8]

        s_const = sem("s_const")
        s_w = [sem(f"s_w{j}") for j in range(4)]
        s_xin = [sem("s_xin0"), sem("s_xin1")]
        s_stored = [sem("s_stored0"), sem("s_stored1")]
        s_ident, s_half, s_adjz = sem("s_ident"), sem("s_half"), sem("s_adjz")
        s_gate_act, s_gate = sem("s_gate_act"), sem("s_gate")
        s_chi, s_clo = sem("s_chi"), sem("s_clo")
        s_ae = sem("s_ae")
        s_wov = sem("s_wov")
        s_bn = [sem("s_bn_l0"), sem("s_bn_l1")]
        s_mv = [sem("s_mv_l0"), sem("s_mv_l1")]
        s_var = [sem("s_var_l0"), sem("s_var_l1")]
        s_rstd = [sem("s_rstd_l0"), sem("s_rstd_l1")]
        s_nmr = [sem("s_nmr_l0"), sem("s_nmr_l1")]
        s_h = sem("s_h")
        s_hhi = sem("s_hhi")
        s_hlo = sem("s_hlo")
        s_ha = sem("s_ha")
        s_hab = sem("s_hab")
        s_qk = sem("s_qk")
        s_hahi, s_halo = sem("s_hahi"), sem("s_halo")
        s_qtop = sem("s_qtop")
        s_qt = sem("s_qt")
        s_qmax = sem("s_qmax")
        s_arg = sem("s_arg")
        s_cols = sem("s_cols")
        s_vt = sem("s_vt")
        s_vrow = sem("s_vrow")
        s_pf = sem("s_pf")
        s_phi, s_plo = sem("s_phi"), sem("s_plo")
        s_part = sem("s_part")
        s_num = sem("s_num")
        s_tt = sem("s_tt")
        s_zsum = sem("s_zsum")
        s_zinv = sem("s_zinv")
        s_rzt = sem("s_rzt")
        s_rz = sem("s_rz")
        s_y = sem("s_y")
        s_x1 = sem("s_x1")
        s_h2 = sem("s_h2")
        s_keep = sem("s_keep")
        s_ht = sem("s_ht")
        s_hthi, s_htlo = sem("s_hthi"), sem("s_htlo")
        s_zl, s_zg = sem("s_zl"), sem("s_zg")
        s_zhi, s_zlo = sem("s_zhi"), sem("s_zlo")
        s_v = sem("s_v")
        s_vhi, s_vlo = sem("s_vhi"), sem("s_vlo")
        s_gl, s_gg = sem("s_gl"), sem("s_gg")
        s_glc, s_ggc = sem("s_glc"), sem("s_ggc")
        s_sql, s_sqg = sem("s_sql"), sem("s_sqg")
        s_sqlm = sem("s_sqlm")
        s_rn = sem("s_rn")
        s_bc = sem("s_bc")
        s_rows = sem("s_rows")
        s_mrn = sem("s_mrn")
        s_kl, s_kg = sem("s_kl"), sem("s_kg")
        s_dist = sem("s_dist")
        s_csq = sem("s_csq")
        s_exp = sem("s_exp")
        s_deg = sem("s_deg")
        s_coef = sem("s_coef")
        s_ks = sem("s_ks")
        s_k = sem("s_k")
        s_kt = sem("s_kt")
        s_kthi, s_ktlo = sem("s_kthi"), sem("s_ktlo")
        s_kv = sem("s_kv")
        s_out = sem("s_out")

        block = ctx.enter_context(nc.Block())

        def run(eng, step):
            step(-1, False, True, True)
            step(0, True, True, True)
            with eng.Fori(1, PAIRS - 2) as i:
                step(i, True, True, True)
            step(PAIRS - 2, True, True, False)
            step(PAIRS - 1, True, False, False)

        x_v = x.rearrange("b (t p) n -> b p t n", p=128)
        out_v = out.rearrange("b (t p) n -> b p t n", p=128)

        @block.sync
        def _(sp):
            def load(p, b):
                sp.dma_start(x_in[:, b], x_v[bass.ds(2 * p + b, 1)].rearrange("b p t n -> p (b t) n")
                             ).then_inc(s_xin[b], 16)

            def store(i, b):
                sp.wait_ge(s_out, 4 * i + 2 * b + 2)
                sp.dma_start(out_v[bass.ds(2 * i + b, 1)].rearrange("b p t n -> p (b t) n"), keep[:, b]
                             ).then_inc(s_stored[b], 16)

            load(0, 0)
            sp.dma_start(ae_f, adj_ext.rearrange("(t p) n -> p t n", p=128)).then_inc(s_const, 16)
            sp.dma_start(bm_rows[:], bm.rearrange("(a n) -> a n", a=1).to_broadcast([128, C])).then_inc(s_const, 16)
            sp.dma_start(adjz[:], adj.rearrange("(t p) n -> p t n", p=128)).then_inc(s_const, 16)
            sp.dma_start(gate[:, 0:1], gate_logit.to_broadcast([128, 1])).then_inc(s_const, 16)
            sp.dma_start(sig[:, 0:1], log_sigma.to_broadcast([128, 1])).then_inc(s_const, 16)
            load(0, 1)
            sp.dma_start(keep[:].rearrange("p b t n -> p (b t) n"),
                         w_v.rearrange("(t p) n -> p t n", p=128)).then_inc(s_w[0], 16)
            sp.dma_start(x1[:].rearrange("p b t n -> p (b t) n"),
                         w_o_t.rearrange("(t p) n -> p t n", p=128)).then_inc(s_w[1], 16)
            sp.dma_start(p_f[:], w_lang_t.rearrange("(t p) n -> p t n", p=128)).then_inc(s_w[2], 16)
            sp.wait_ge(s_clo, 1)
            sp.dma_start(keep[:].rearrange("p b t n -> p (b t) n"),
                         w_grav_t.rearrange("(t p) n -> p t n", p=128)).then_inc(s_w[3], 16)

            def step(i, l1, l0, ahead):
                p = i + 1
                for b in range(2):
                    if b and l1:
                        store(i, 0)
                        store(i, 1)
                    if ahead:
                        sp.wait_ge(s_x1, 2 * p + b + 1)
                        load(p + 1, b)

            run(sp, step)
            sp.wait_ge(s_stored[0], 16 * PAIRS)
            sp.wait_ge(s_stored[1], 16 * PAIRS)

        @block.gpsimd
        def _(pool):
            pool.memset(minus_half[:], -0.5).then_inc(s_half, 1)
            pool.memset(ident[:], 0.0).then_inc(s_ident, 1)
            pool.wait_ge(s_ident, 1)
            pool.affine_select(out=ident[:], in_=ident[:], compare_op=ALU.not_equal, fill=1.0, base=0,
                               pattern=[[-1, 128]], channel_multiplier=1).then_inc(s_ident, 1)
            pool.wait_ge(s_const, 16 * 5)
            pool.affine_select(out=adjz[:], in_=adjz[:], compare_op=ALU.not_equal, fill=0.0, base=0,
                               pattern=[[128, CB], [-1, C]], channel_multiplier=1).then_inc(s_adjz, 1)
            pool.wait_ge(s_half, 1)

            def norm_scale(layer, p, b):
                n = 2 * p + b + 1
                j = 2 * layer + b
                pool.wait_ge(s_var[layer], n)
                pool.tensor_tensor(rstd[:, j], var[:, j], minus_half[:], ALU.pow).then_inc(s_rstd[layer], 1)
                pool.wait_ge(s_rstd[layer], n)
                pool.tensor_tensor(nmr[:, j], nmean[:, j], rstd[:, j], ALU.mult).then_inc(s_nmr[layer], 1)

            def h_low(p, b):
                pool.wait_ge(s_hhi, 2 * p + b + 1)
                pool.wait_ge(s_ha, 8 * p + 4 * b)
                pool.tensor_tensor(h_lo[:], h[:], h_hi[:].bitcast(fp32), ALU.subtract).then_inc(s_hlo, 1)

            def p_total(p, b):
                n = 6 * p + 3 * b
                pool.wait_ge(s_pf, 8 * p + 4 * b + 2)
                pool.wait_ge(s_tt, 2 * p + b)
                pool.tensor_tensor(p_sum[:], p_f[:, 0], p_f[:, 1], ALU.add).then_inc(s_part, 1)
                for j in range(2, NB):
                    pool.wait_ge(s_pf, 8 * p + 4 * b + j + 1)
                    pool.wait_ge(s_part, n + j - 1)
                    pool.tensor_tensor(p_sum[:], p_sum[:], p_f[:, j], ALU.add).then_inc(s_part, 1)

            def step(i, l1, l0, ahead):
                p = i + 1
                if l0:
                    norm_scale(0, p, 1)
                    h_low(p, 1)
                    p_total(p, 0)
                if l1:
                    for b in range(2):
                        pool.wait_ge(s_sqlm, 2 * i + b + 1)
                        pool.tensor_tensor(r_norm[:, b], sq_lm[:, b], minus_half[:], ALU.pow).then_inc(s_rn, 1)
                if l0:
                    p_total(p, 1)
                if l1:
                    for b in range(2):
                        pool.wait_ge(s_rows, 2 * i + b + 1)
                        for t in range(CB):
                            last = pool.tensor_tensor(k_f[:, b, t], adjz[:, t], rows[:, b, 0], ALU.mult)
                        last.then_inc(s_mrn, 1)
                if l0:
                    norm_scale(1, p, 0)
                    norm_scale(1, p, 1)
                if ahead:
                    norm_scale(0, p + 1, 0)
                    h_low(p + 1, 0)

            norm_scale(0, 0, 0)
            h_low(0, 0)
            run(pool, step)

        @block.scalar
        def _(act):
            def copy(o, i):
                return act.activation(o, i, ACT.Copy)

            act.wait_ge(s_const, 16 * 5)
            copy(ae_hi[:], ae_f).then_inc(s_ae, 1)
            act.activation(gate[:, 1:2], gate[:, 0:1], ACT.Exp, scale=-1.0).then_inc(s_gate_act, 1)
            act.activation(sig[:, 1:2], sig[:, 0:1], ACT.Exp).then_inc(s_gate_act, 1)

            def h_make(p, b):
                n = 2 * p + b
                act.wait_ge(s_xin[b], 16 * p + 16)
                act.wait_ge(s_nmr[0], n + 1)
                act.wait_ge(s_hlo, n)
                for t in range(CB):
                    last = act.activation(h[:, t], x_in[:, b, t], ACT.Relu, scale=rstd[:, b, t:t + 1],
                                          bias=nmr[:, b, t:t + 1])
                last.then_inc(s_h, 1)
                act.wait_ge(s_h, n + 1)
                act.wait_ge(s_ha, 8 * p + 4 * b)
                copy(h_hi[:], h[:]).then_inc(s_hhi, 1)

            def ha_high(p, b):
                for j in range(NB):
                    act.wait_ge(s_hab, 8 * p + 4 * b + j + 1)
                    copy(ha_hi[:, b, j], hab[:, j % 2]).then_inc(s_hahi, 1)

            def columns(p, b):
                act.wait_ge(s_arg, 2 * p + b + 1)
                act.activation(col_v[:, b], k_pos[:, b], ACT.Exp, scale=SLOPE - 1.0)
                act.activation(col_a[:, b], q_less[:, b], ACT.Exp)
                act.activation(col_b[:, b], q_less[:, b], ACT.Exp, scale=SLOPE).then_inc(s_cols, 1)

            def v_rows(p, b):
                act.wait_ge(s_vt, 2 * p + b + 1)
                act.wait_ge(s_pf, 8 * p + 4 * b)
                copy(v_row[:], L0_BANK[1][:]).then_inc(s_vrow, 1)

            def p_high(p, b):
                act.wait_ge(s_num, 4 * p + 2 * b)
                for j in range(NB):
                    act.wait_ge(s_pf, 8 * p + 4 * b + j + 1)
                    copy(p_hi[:, j], p_f[:, j]).then_inc(s_phi, 1)

            def rz_rows(p, b):
                act.wait_ge(s_rzt, 2 * p + b + 1)
                act.wait_ge(s_y, 4 * p + 2 * b)
                copy(rz_row[:], L0_BANK[1][:]).then_inc(s_rz, 1)

            def h2_make(p, b):
                act.wait_ge(s_nmr[1], 2 * p + b + 1)
                act.wait_ge(s_x1, 2 * p + b + 1)
                act.wait_ge(s_ht, 4 * p)
                for t in range(CB):
                    last = act.activation(h2[:, b, t], x1[:, b, t], ACT.Relu, scale=rstd[:, 2 + b, t:t + 1],
                                          bias=nmr[:, 2 + b, t:t + 1])
                last.then_inc(s_h2, 1)

            def ht_high(i):
                for f in range(2 * CB):
                    act.wait_ge(s_ht, 4 * i + f + 1)
                    act.wait_ge(s_v, 4 * i)
                    act.wait_ge(s_zg, 4 * i)
                    copy(ht_hi[:, :, f * 128:(f + 1) * 128],
                         L1_BANK[f][:].rearrange("p (t n) -> p t n", t=NB)).then_inc(s_hthi, 1)

            def z_high(i, kind, e, s_z, psum):
                act.wait_ge(s_z, 4 * i + e + 1)
                if kind == 0:
                    act.wait_ge(s_gg, 2 * i)
                else:
                    act.wait_ge(s_gl, 2 * i + 2)
                copy(z_hi[:, e], psum[:]).then_inc(s_zhi, 1)

            def v_high(i, f):
                act.wait_ge(s_v, 4 * i + f + 1)
                act.wait_ge(s_kv, 4 * i)
                copy(v_hi[:, f], L1_BANK[f][:]).then_inc(s_vhi, 1)

            def step(i, l1, l0, ahead):
                p = i + 1
                if l0:
                    ha_high(p, 0)
                if l1:
                    ht_high(i)
                    for b in range(2):
                        act.wait_ge(s_x1, 2 * i + b + 1)
                        act.wait_ge(s_stored[b], 16 * i)
                        copy(keep[:, b], x1[:, b]).then_inc(s_keep, 1)
                if l0:
                    h_make(p, 1)
                if l1:
                    for e in range(NB):
                        z_high(i, 0, e, s_zl, L1_BANK[e])
                if l0:
                    columns(p, 0)
                if l1:
                    v_high(i, 0)
                    v_high(i, 1)
                if l0:
                    v_rows(p, 0)
                    p_high(p, 0)
                if l1:
                    v_high(i, 2)
                    v_high(i, 3)
                if l0:
                    ha_high(p, 1)
                if l1:
                    for b in range(2):
                        act.wait_ge(s_gl, 2 * i + b + 1)
                        act.wait_ge(s_kl, 4 * i)
                        copy(g_l[:, b].rearrange("p t n -> p (t n)"), L1_BANK[b][:]).then_inc(s_glc, 1)
                    z_high(i, 1, 0, s_zg, L1_BANK[2])
                    z_high(i, 1, 1, s_zg, L1_BANK[3])
                if l0:
                    columns(p, 1)
                if l1:
                    z_high(i, 1, 2, s_zg, L1_BANK[0])
                    z_high(i, 1, 3, s_zg, L1_BANK[1])
                if l0:
                    v_rows(p, 1)
                    p_high(p, 1)
                if l1:
                    act.wait_ge(s_gg, 2 * i + 1)
                    act.wait_ge(s_k, 4 * i)
                    copy(g_g[:, 0].rearrange("p t n -> p (t n)"), L1_BANK[2][:]).then_inc(s_ggc, 1)
                if l0:
                    rz_rows(p, 0)
                if l1:
                    act.wait_ge(s_gg, 2 * i + 2)
                    copy(g_g[:, 1].rearrange("p t n -> p (t n)"), L1_BANK[3][:]).then_inc(s_ggc, 1)
                    for b in range(2):
                        act.wait_ge(s_bc, 2 * i + b + 1)
                        act.wait_ge(s_mrn, 2 * i)
                        act.wait_ge(s_dist, 2 * i)
                        copy(rows[:, b].rearrange("p t n -> p (t n)"), L1_BANK[b][:]).then_inc(s_rows, 1)
                    for b in range(2):
                        act.wait_ge(s_dist, 2 * i + b + 1)
                        act.wait_ge(s_csq, 2 * i + b + 1)
                        act.wait_ge(s_gate, 7)
                        for t in range(CB):
                            act.activation(g_g[:, b, t], g_g[:, b, t], ACT.Exp, scale=sig[:, 4:5],
                                           bias=c_sq[:, b, t:t + 1]).then_inc(s_exp, 1)
                if l0:
                    h2_make(p, 0)
                if l1:
                    act.wait_ge(s_kt, 2 * i + 1)
                    act.wait_ge(s_kv, 4 * i)
                    copy(kt_hi[:, 0].rearrange("p t n -> p (t n)"), L1_BANK[2][:]).then_inc(s_kthi, 1)
                if l0:
                    rz_rows(p, 1)
                if l1:
                    act.wait_ge(s_kt, 2 * i + 2)
                    copy(kt_hi[:, 1].rearrange("p t n -> p (t n)"), L1_BANK[3][:]).then_inc(s_kthi, 1)
                if l0:
                    h2_make(p, 1)
                if ahead:
                    h_make(p + 1, 0)

            h_make(0, 0)
            act.wait_ge(s_w[0], 16)
            copy(z_hi[:], keep[:].rearrange("p b t n -> p (b t) n")).then_inc(s_chi, 1)
            act.wait_ge(s_w[1], 16)
            copy(v_hi[:], x1[:].rearrange("p b t n -> p (b t) n")).then_inc(s_chi, 1)
            act.wait_ge(s_w[2], 16)
            copy(wl_hi[:], p_f[:]).then_inc(s_chi, 1)
            act.wait_ge(s_w[3], 16)
            copy(wg_hi[:], keep[:].rearrange("p b t n -> p (b t) n")).then_inc(s_chi, 1)
            for d in range(NB):
                act.wait_ge(s_wov, d + 1)
                copy(wov_hi[:, d], L1_BANK[d][:]).then_inc(s_chi, 1)
            run(act, step)

        @block.tensor
        def _(pe):
            def three(o, a_hi, a_lo, b_hi, b_lo, first, last):
                pe.matmul(o, a_hi, b_hi, start=first, stop=False)
                pe.matmul(o, a_hi, b_lo, start=False, stop=False)
                return pe.matmul(o, a_lo, b_hi, start=False, stop=last)

            def column_to_row(o, col):
                return pe.transpose(o, col.to_broadcast([128, 128]), ident[:])

            def adj_h(p, b):
                pe.wait_ge(s_hlo, 2 * p + b + 1)
                pe.wait_ge(s_hhi, 2 * p + b + 1)
                for j in range(NB):
                    if j == 0:
                        pe.wait_ge(s_qmax if b else s_zsum, 2 * p + b)
                    elif j == 1:
                        pe.wait_ge(s_vrow if b else s_rz, 2 * p + b)
                    else:
                        pe.wait_ge(s_hab, 8 * p + 4 * b + j - 1)
                        pe.wait_ge(s_qk, 8 * p + 4 * b + j - 1)
                    for t in range(CB):
                        m = slice(j * 128, (j + 1) * 128)
                        mm = three(L0_BANK[j % 2][:, 0:CE], h_hi[:, t, m], h_lo[:, t, m],
                                   ae_hi[:, t], ae_lo[:, t], t == 0, t == CB - 1)
                    mm.then_inc(s_ha, 1)

            def q_row(p, b):
                pe.wait_ge(s_qtop, 2 * p + b + 1)
                column_to_row(L0_BANK[0][:, 0:128], q_top[:, b:b + 1]).then_inc(s_qt, 1)

            def v_to_row(p, b):
                pe.wait_ge(s_cols, 2 * p + b + 1)
                for j in range(NB):
                    mm = column_to_row(L0_BANK[1][:, j * 128:(j + 1) * 128], col_v[:, b, j:j + 1])
                mm.then_inc(s_vt, 1)

            def attend(i, p, b, l1):
                if b:
                    pe.wait_ge(s_y, 4 * p + 2)
                elif l1:
                    pe.wait_ge(s_out, 4 * i)
                for o in range(CB):
                    for j in range(NB):
                        if o == 0:
                            pe.wait_ge(s_phi, 8 * p + 4 * b + j + 1)
                            pe.wait_ge(s_plo, 8 * p + 4 * b + j + 1)
                            pe.wait_ge(s_halo, 8 * p + 4 * b + j + 1)
                        m = slice(o * 128, (o + 1) * 128)
                        mm = three(SUM_BANK[o][:], ha_hi[:, b, j, m], ha_lo[:, b, j, m],
                                   p_hi[:, j], p_lo[:, j], j == 0, j == NB - 1)
                    mm.then_inc(s_num, 1)
                pe.wait_ge(s_part, 6 * p + 3 * b + 3)
                pe.wait_ge(s_zsum if b else s_qmax, 2 * p + 1 if b else 2 * p + 2)
                for j in range(NB):
                    mm = pe.transpose(L0_BANK[0][:, j * 128:(j + 1) * 128], p_sum[:, j * 128:(j + 1) * 128], ident[:])
                mm.then_inc(s_tt, 1)

            def rz_to_row(p, b):
                pe.wait_ge(s_zinv, 2 * p + b + 1)
                pe.wait_ge(s_rz if b else s_vrow, 2 * p + 1 if b else 2 * p + 2)
                for j in range(NB):
                    mm = column_to_row(L0_BANK[1][:, j * 128:(j + 1) * 128], z_inv[:, b, j:j + 1])
                mm.then_inc(s_rzt, 1)

            def h2_transpose(i):
                for f in range(2 * CB):
                    b, t = divmod(f, CB)
                    pe.wait_ge(s_h2, 2 * i + b + 1)
                    pe.wait_ge(s_rows if b == 0 else s_ktlo, 2 * i)
                    for d in range(NB):
                        mm = pe.transpose(L1_BANK[f][:, d * 128:(d + 1) * 128],
                                          h2[:, b, t, d * 128:(d + 1) * 128], ident[:])
                    mm.then_inc(s_ht, 1)

            def z_block(i, e, hi, lo, psum, s_z):
                m = slice(e * 128, (e + 1) * 128)
                for d in range(NB):
                    mm = three(psum[:], hi[:, d, m], lo[:, d, m], ht_hi[:, d], ht_lo[:, d], d == 0, d == NB - 1)
                mm.then_inc(s_z, 1)

            def v_block(i, f):
                pe.wait_ge(s_zlo, 8 * i + f + 1)
                m = slice(f * 128, (f + 1) * 128)
                for d in range(NB):
                    mm = three(L1_BANK[f][:], ht_hi[:, d, m], ht_lo[:, d, m], wov_hi[:, d], wov_lo[:, d],
                               d == 0, d == NB - 1)
                mm.then_inc(s_v, 1)

            def gram(i, b, psum, s_g):
                for t in range(CB):
                    o = psum[:, t * C:(t + 1) * C]
                    m = slice(b * C + t * 128, b * C + (t + 1) * 128)
                    n = slice(b * C, (b + 1) * C)
                    for e in range(NB):
                        mm = three(o, z_hi[:, e, m], z_lo[:, e, m], z_hi[:, e, n], z_lo[:, e, n],
                                   e == 0, e == NB - 1)
                mm.then_inc(s_g, 1)

            def rows_of(i, b):
                pe.wait_ge(s_zlo, 8 * i + 7 + b)
                pe.wait_ge(s_rn, 2 * i + b + 1)
                pe.wait_ge(s_sqg, 4 * i + 2 * b + 2)
                for t in range(CB):
                    column_to_row(L1_BANK[b][:, t * 128:(t + 1) * 128], r_norm[:, b, t:t + 1])
                    mm = column_to_row(L1_BANK[b][:, C + t * 128:C + (t + 1) * 128], sq_g[:, b, t:t + 1])
                mm.then_inc(s_bc, 1)

            def k_transpose(i, b):
                pe.wait_ge(s_ggc, 2 * i + b + 1)
                pe.wait_ge(s_k, 4 * i + 2 * b + 2)
                for mb in range(CB):
                    for t in range(CB):
                        mm = pe.transpose(L1_BANK[2 + b][:, mb * C + t * 128:mb * C + (t + 1) * 128],
                                          k_f[:, b, t, mb * 128:(mb + 1) * 128], ident[:])
                mm.then_inc(s_kt, 1)

            def mix(i, b, l0):
                if b == 0 and l0:
                    pe.wait_ge(s_y, 4 * i + 8)
                if b == 1:
                    pe.wait_ge(s_out, 4 * i + 2)
                pe.wait_ge(s_ktlo, 2 * i + b + 1)
                for t in range(CB):
                    for mb in range(CB):
                        n = slice(t * 128, (t + 1) * 128)
                        mm = three(SUM_BANK[t][:], kt_hi[:, b, mb, n], kt_lo[:, b, mb, n],
                                   v_hi[:, 2 * b + mb], v_lo[:, 2 * b + mb], mb == 0, mb == CB - 1)
                    mm.then_inc(s_kv, 1)

            def step(i, l1, l0, ahead):
                p = i + 1
                if l0:
                    adj_h(p, 0)
                if l1:
                    h2_transpose(i)
                    pe.wait_ge(s_htlo, 4 * i + 4)
                    for e in range(NB):
                        z_block(i, e, wl_hi, wl_lo, L1_BANK[e], s_zl)
                if l0:
                    q_row(p, 0)
                if l1:
                    v_block(i, 0)
                    v_block(i, 1)
                if l0:
                    v_to_row(p, 0)
                if l1:
                    v_block(i, 2)
                    v_block(i, 3)
                if l0:
                    adj_h(p, 1)
                if l1:
                    for b in range(2):
                        pe.wait_ge(s_vlo, 4 * i + b + 1)
                        gram(i, b, L1_BANK[b], s_gl)
                    pe.wait_ge(s_vlo, 4 * i + 3)
                    z_block(i, 0, wg_hi, wg_lo, L1_BANK[2], s_zg)
                    pe.wait_ge(s_vlo, 4 * i + 4)
                    z_block(i, 1, wg_hi, wg_lo, L1_BANK[3], s_zg)
                if l0:
                    q_row(p, 1)
                if l1:
                    pe.wait_ge(s_glc, 2 * i + 1)
                    z_block(i, 2, wg_hi, wg_lo, L1_BANK[0], s_zg)
                    pe.wait_ge(s_glc, 2 * i + 2)
                    z_block(i, 3, wg_hi, wg_lo, L1_BANK[1], s_zg)
                if l0:
                    v_to_row(p, 1)
                    attend(i, p, 0, l1)
                if l1:
                    pe.wait_ge(s_zlo, 8 * i + 8)
                    gram(i, 0, L1_BANK[2], s_gg)
                if l0:
                    rz_to_row(p, 0)
                if l1:
                    gram(i, 1, L1_BANK[3], s_gg)
                    rows_of(i, 0)
                    rows_of(i, 1)
                if l0:
                    attend(i, p, 1, l1)
                if l1:
                    k_transpose(i, 0)
                if l0:
                    rz_to_row(p, 1)
                if l1:
                    k_transpose(i, 1)
                    mix(i, 0, l0)
                    mix(i, 1, l0)

            pe.wait_ge(s_ident, 2)
            pe.wait_ge(s_ae, 2)
            pe.wait_ge(s_chi, 2)
            pe.wait_ge(s_clo, 2)
            for d in range(NB):
                m = slice(d * 128, (d + 1) * 128)
                for k in range(NB):
                    mm = three(L1_BANK[d][:], z_hi[:, k, m], z_lo[:, k, m], v_hi[:, k], v_lo[:, k],
                               k == 0, k == NB - 1)
                mm.then_inc(s_wov, 1)
            run(pe, step)

        @block.vector
        def _(dve):
            def minus_hi(o, f, hi):
                return dve.tensor_tensor(o, f, hi.bitcast(fp32), ALU.subtract)

            def stats(layer, src, p, b):
                n, j = 2 * p + b, 2 * layer + b
                if layer == 0:
                    dve.wait_ge(s_xin[b], 16 * p + 16)
                    if not isinstance(p, int) or p > 0:
                        dve.wait_ge(s_h, 2 * p + b - 1)
                else:
                    dve.wait_ge(s_x1, n + 1)
                    dve.wait_ge(s_h2, 2 * p)
                for t in range(CB):
                    dve.bn_stats(bn[:, j, t], src[:, b, t]).then_inc(s_bn[layer], 1)
                dve.wait_ge(s_bn[layer], 2 * n + 2)
                dve.tensor_tensor(mv[:, j, 0], bn[:, j, :, 1], bn[:, j, :, 4], ALU.add)
                dve.tensor_tensor(mv[:, j, 1], bn[:, j, :, 1], bn[:, j, :, 4], ALU.subtract)
                dve.tensor_tensor(mv[:, j, 2], bn[:, j, :, 2], bn[:, j, :, 5], ALU.add).then_inc(s_mv[layer], 1)
                dve.wait_ge(s_mv[layer], 2 * n + 1)
                dve.tensor_scalar(nmean[:, j], mv[:, j, 0], -0.5, None, ALU.mult)
                dve.scalar_tensor_tensor(out=mv[:, j, 3], in0=mv[:, j, 1], scalar=0.25, in1=mv[:, j, 1],
                                         op0=ALU.mult, op1=ALU.mult)
                dve.tensor_scalar(mv[:, j, 4], mv[:, j, 2], 1.0 / N, LN_EPS, ALU.mult, ALU.add
                                  ).then_inc(s_mv[layer], 1)
                dve.wait_ge(s_mv[layer], 2 * n + 2)
                dve.tensor_tensor(var[:, j], mv[:, j, 3], mv[:, j, 4], ALU.add).then_inc(s_var[layer], 1)

            def ha_drain(p, b):
                def low(j):
                    n = 8 * p + 4 * b + j + 1
                    dve.wait_ge(s_hahi, n)
                    minus_hi(ha_lo[:, b, j], hab[:, j % 2], ha_hi[:, b, j]).then_inc(s_halo, 1)

                for j in range(NB):
                    n = 8 * p + 4 * b + j + 1
                    dve.wait_ge(s_ha, n)
                    if j >= 2:
                        dve.wait_ge(s_halo, n - 2)
                    dve.tensor_tensor(hab[:, j % 2], L0_BANK[j % 2][:, 0:C], bm_rows[:], ALU.add).then_inc(s_hab, 1)
                    dve.tensor_copy(qk[:, b, j], L0_BANK[j % 2][:, C:CE]).then_inc(s_qk, 1)
                    if j >= 1:
                        low(j - 1)
                low(NB - 1)
                dve.wait_ge(s_qk, 8 * p + 4 * b + 4)
                dve.tensor_reduce(q_top[:, b:b + 1], qk[:, b, :, 0], AX.X, ALU.max).then_inc(s_qtop, 1)

            def arguments(p, b):
                n = 2 * p + b + 1
                dve.wait_ge(s_qt, n)
                dve.tensor_reduce(q_max[:, b:b + 1], L0_BANK[0][:, 0:128], AX.X, ALU.max).then_inc(s_qmax, 1)
                dve.wait_ge(s_qmax, n)
                dve.tensor_scalar(q_less[:, b], qk[:, b, :, 0], q_max[:, b:b + 1], None, ALU.subtract)
                dve.tensor_scalar(k_pos[:, b], qk[:, b, :, 1], q_max[:, b:b + 1], 0.0, ALU.add, ALU.max
                                  ).then_inc(s_arg, 1)

            def p_make(p, b):
                dve.wait_ge(s_vrow, 2 * p + b + 1)
                dve.wait_ge(s_phi, 8 * p + 4 * b)
                dve.wait_ge(s_plo, 8 * p + 4 * b)
                dve.wait_ge(s_part, 6 * p + 3 * b)
                for j in range(NB):
                    dve.tensor_scalar(p_f[:, j], v_row[:], col_b[:, b, j:j + 1], col_a[:, b, j:j + 1],
                                      ALU.mult, ALU.max).then_inc(s_pf, 1)

            def p_low(p, b):
                dve.wait_ge(s_num, 4 * p + 2 * b)
                for j in range(NB):
                    dve.wait_ge(s_phi, 8 * p + 4 * b + j + 1)
                    minus_hi(p_lo[:, j], p_f[:, j], p_hi[:, j]).then_inc(s_plo, 1)

            def z_column(p, b):
                n = 2 * p + b + 1
                dve.wait_ge(s_tt, n)
                dve.tensor_reduce(z_sum[:, b], L0_BANK[0][:].rearrange("p (t n) -> p t n", t=NB), AX.X, ALU.add
                                  ).then_inc(s_zsum, 1)
                dve.wait_ge(s_zsum, n)
                dve.reciprocal(z_inv[:, b], z_sum[:, b]).then_inc(s_zinv, 1)

            def residual(p, b):
                n = 2 * p + b
                dve.wait_ge(s_rz, n + 1)
                dve.wait_ge(s_keep, 2 * p)
                for o in range(CB):
                    dve.wait_ge(s_num, 2 * n + o + 1)
                    dve.scalar_tensor_tensor(out=x1[:, b, o], in0=SUM_BANK[o][:], scalar=0.0, in1=rz_row[:],
                                             op0=ALU.max, op1=ALU.mult).then_inc(s_y, 1)
                dve.wait_ge(s_y, 2 * n + 2)
                dve.tensor_tensor(x1[:, b], x1[:, b], x_in[:, b], ALU.add).then_inc(s_x1, 1)

            def ht_low(i):
                for f in range(2 * CB):
                    dve.wait_ge(s_hthi, 4 * i + f + 1)
                    m = slice(f * 128, (f + 1) * 128)
                    minus_hi(ht_lo[:, :, m], L1_BANK[f][:].rearrange("p (t n) -> p t n", t=NB),
                             ht_hi[:, :, m]).then_inc(s_htlo, 1)

            def z_low(i, kind, e, psum):
                dve.wait_ge(s_zhi, 8 * i + 4 * kind + e + 1)
                minus_hi(z_lo[:, e], psum[:], z_hi[:, e]).then_inc(s_zlo, 1)

            def v_low(i, f):
                dve.wait_ge(s_vhi, 4 * i + f + 1)
                minus_hi(v_lo[:, f], L1_BANK[f][:], v_hi[:, f]).then_inc(s_vlo, 1)

            def diagonal(i, b, g, s_copied, sq, s_sq, first):
                dve.wait_ge(s_copied, 2 * i + b + 1)
                for t in range(CB):
                    n = 4 * i + 2 * b + t
                    dve.wait_ge(s_sq, n)
                    if first is not None and b == 0 and t == 0:
                        dve.wait_ge(*first)
                    dve.scalar_tensor_tensor(out=junk[:], in0=g[:, b, t, t * 128:(t + 1) * 128], scalar=1.0,
                                             in1=ident[:], op0=ALU.mult, op1=ALU.mult,
                                             accum_out=sq[:, b, t:t + 1]).then_inc(s_sq, 1)

            def kernels_raw(i, b):
                dve.wait_ge(s_mrn, 2 * i + b + 1)
                for t in range(CB):
                    dve.scalar_tensor_tensor(out=k_f[:, b, t], in0=g_l[:, b, t], scalar=0.0, in1=k_f[:, b, t],
                                             op0=ALU.max, op1=ALU.mult,
                                             accum_out=deg[:, b, 0, t:t + 1]).then_inc(s_kl, 1)

            def distances(i, b):
                dve.wait_ge(s_rows, 2 * i + b + 1)
                dve.wait_ge(s_sqg, 4 * i + 2 * b + 2)
                for t in range(CB):
                    last = dve.scalar_tensor_tensor(out=g_g[:, b, t], in0=g_g[:, b, t], scalar=-2.0,
                                                    in1=rows[:, b, 1], op0=ALU.mult, op1=ALU.add)
                last.then_inc(s_dist, 1)
                dve.tensor_scalar(c_sq[:, b], sq_g[:, b], sig[:, 4:5], None, ALU.mult).then_inc(s_csq, 1)

            def kernels(i, b):
                n = 4 * i + 2 * b
                for t in range(CB):
                    dve.wait_ge(s_exp, n + t + 1)
                    dve.scalar_tensor_tensor(out=g_g[:, b, t], in0=g_g[:, b, t], scalar=1.0, in1=adjz[:, t],
                                             op0=ALU.min, op1=ALU.mult,
                                             accum_out=deg[:, b, 1, t:t + 1]).then_inc(s_kg, 1)
                dve.wait_ge(s_kl, n + 2)
                dve.wait_ge(s_kg, n + 2)
                dve.tensor_tensor(deg2[:, b, 0], deg[:, b, 0], r_norm[:, b], ALU.mult)
                dve.tensor_copy(deg2[:, b, 1], deg[:, b, 1]).then_inc(s_deg, 1)
                dve.wait_ge(s_deg, 6 * i + 3 * b + 1)
                dve.tensor_scalar(deg3[:, b], deg2[:, b], TINY, None, ALU.max).then_inc(s_deg, 1)
                dve.wait_ge(s_deg, 6 * i + 3 * b + 2)
                dve.reciprocal(deg_inv[:, b], deg3[:, b]).then_inc(s_deg, 1)
                dve.wait_ge(s_deg, 6 * i + 3 * b + 3)
                dve.scalar_tensor_tensor(out=coef[:, b, 0], in0=deg_inv[:, b, 0], scalar=gate[:, 3:4],
                                         in1=r_norm[:, b], op0=ALU.mult, op1=ALU.mult)
                dve.tensor_scalar(coef[:, b, 1], deg_inv[:, b, 1], gate[:, 4:5], None, ALU.mult
                                  ).then_inc(s_coef, 1)
                dve.wait_ge(s_coef, 2 * i + b + 1)
                for t in range(CB):
                    dve.tensor_scalar(k_f[:, b, t], k_f[:, b, t], coef[:, b, 0, t:t + 1], None, ALU.mult
                                      ).then_inc(s_ks, 1)
                for t in range(CB):
                    dve.wait_ge(s_ks, n + t + 1)
                    dve.scalar_tensor_tensor(out=k_f[:, b, t], in0=g_g[:, b, t], scalar=coef[:, b, 1, t:t + 1],
                                             in1=k_f[:, b, t], op0=ALU.mult, op1=ALU.add).then_inc(s_k, 1)

            def kt_low(i, b):
                dve.wait_ge(s_kthi, 2 * i + b + 1)
                minus_hi(kt_lo[:, b].rearrange("p t n -> p (t n)"), L1_BANK[2 + b][:],
                         kt_hi[:, b].rearrange("p t n -> p (t n)")).then_inc(s_ktlo, 1)

            def output(i, b):
                dve.wait_ge(s_keep, 2 * i + b + 1)
                for t in range(CB):
                    dve.wait_ge(s_kv, 4 * i + 2 * b + t + 1)
                    dve.tensor_tensor(keep[:, b, t], SUM_BANK[t][:], keep[:, b, t], ALU.add).then_inc(s_out, 1)

            def step(i, l1, l0, ahead):
                p = i + 1
                if l0:
                    ha_drain(p, 0)
                if l1:
                    ht_low(i)
                if l0:
                    stats(0, x_in, p, 1)
                if l1:
                    for e in range(NB):
                        z_low(i, 0, e, L1_BANK[e])
                if l0:
                    arguments(p, 0)
                if l1:
                    v_low(i, 0)
                    v_low(i, 1)
                if l0:
                    p_make(p, 0)
                    p_low(p, 0)
                if l1:
                    v_low(i, 2)
                    v_low(i, 3)
                if l0:
                    ha_drain(p, 1)
                if l1:
                    for b in range(2):
                        diagonal(i, b, g_l, s_glc, sq_l, s_sql, (s_sqg, 4 * i))
                        dve.wait_ge(s_sql, 4 * i + 2 * b + 2)
                        dve.tensor_scalar(sq_lm[:, b], sq_l[:, b], TINY * TINY, None, ALU.max
                                          ).then_inc(s_sqlm, 1)
                    z_low(i, 1, 0, L1_BANK[2])
                    z_low(i, 1, 1, L1_BANK[3])
                if l0:
                    arguments(p, 1)
                if l1:
                    z_low(i, 1, 2, L1_BANK[0])
                    z_low(i, 1, 3, L1_BANK[1])
                if l0:
                    p_make(p, 1)
                    z_column(p, 0)
                    p_low(p, 1)
                if l1:
                    diagonal(i, 0, g_g, s_ggc, sq_g, s_sqg, (s_sql, 4 * i + 4))
                if l0:
                    residual(p, 0)
                if l1:
                    diagonal(i, 1, g_g, s_ggc, sq_g, s_sqg, None)
                    for b in range(2):
                        distances(i, b)
                        kernels_raw(i, b)
                    kernels(i, 0)
                    kernels(i, 1)
                if l0:
                    stats(1, x1, p, 0)
                    z_column(p, 1)
                if l1:
                    kt_low(i, 0)
                if l0:
                    residual(p, 1)
                if l1:
                    kt_low(i, 1)
                if l0:
                    stats(1, x1, p, 1)
                if l1:
                    output(i, 0)
                if ahead:
                    stats(0, x_in, p + 1, 0)
                if l1:
                    output(i, 1)

            stats(0, x_in, 0, 0)
            dve.wait_ge(s_ae, 1)
            minus_hi(ae_lo[:], ae_f, ae_hi[:]).then_inc(s_ae, 1)
            dve.wait_ge(s_gate_act, 2)
            dve.tensor_scalar(gate[:, 2:3], gate[:, 1:2], 1.0, None, ALU.add).then_inc(s_gate, 1)
            dve.tensor_scalar(sig[:, 2:3], sig[:, 1:2], sig[:, 1:2], 2.0, ALU.mult, ALU.mult).then_inc(s_gate, 1)
            dve.wait_ge(s_gate, 2)
            dve.reciprocal(gate[:, 3:4], gate[:, 2:3]).then_inc(s_gate, 1)
            dve.reciprocal(sig[:, 3:4], sig[:, 2:3]).then_inc(s_gate, 1)
            dve.wait_ge(s_gate, 4)
            dve.tensor_scalar(gate[:, 4:5], gate[:, 3:4], -1.0, 1.0, ALU.mult, ALU.add).then_inc(s_gate, 1)
            dve.tensor_scalar(sig[:, 4:5], sig[:, 3:4], -1.0, None, ALU.mult).then_inc(s_gate, 1)
            dve.wait_ge(s_gate, 6)
            dve.wait_ge(s_adjz, 1)
            dve.tensor_copy(gate[:, 5:6], gate[:, 4:5]).then_inc(s_gate, 1)
            dve.wait_ge(s_chi, 1)
            minus_hi(z_lo[:], keep[:].rearrange("p b t n -> p (b t) n"), z_hi[:]).then_inc(s_clo, 1)
            dve.wait_ge(s_chi, 2)
            minus_hi(v_lo[:], x1[:].rearrange("p b t n -> p (b t) n"), v_hi[:]).then_inc(s_clo, 1)
            dve.wait_ge(s_chi, 3)
            minus_hi(wl_lo[:], p_f[:], wl_hi[:]).then_inc(s_clo, 1)
            dve.wait_ge(s_chi, 4)
            minus_hi(wg_lo[:], keep[:].rearrange("p b t n -> p (b t) n"), wg_hi[:]).then_inc(s_clo, 1)
            for d in range(NB):
                dve.wait_ge(s_chi, 5 + d)
                minus_hi(wov_lo[:, d], L1_BANK[d][:], wov_hi[:, d]).then_inc(s_clo, 1)
            run(dve, step)


def kernel(x, adj, L0_gnn_wq, L0_gnn_wk, L0_gnn_bm, L1_gnn_W_lang, L1_gnn_W_grav, L1_gnn_W_V, L1_gnn_W_O,
           L1_gnn_gate_logit, L1_gnn_log_sigma):
    import numpy as np
    import concourse.bacc as bacc
    from concourse.bass_utils import run_bass_kernel_spmd

    arrays = {
        "x": np.ascontiguousarray(x),
        "adj": np.ascontiguousarray(adj),
        "adj_ext": np.concatenate([np.asarray(adj).T, np.asarray(L0_gnn_wq)[:, None],
                                   np.asarray(L0_gnn_wk)[:, None]], axis=1),
        "bm": np.ascontiguousarray(L0_gnn_bm),
        "w_lang_t": np.ascontiguousarray(np.asarray(L1_gnn_W_lang).T),
        "w_grav_t": np.ascontiguousarray(np.asarray(L1_gnn_W_grav).T),
        "w_v": np.ascontiguousarray(L1_gnn_W_V),
        "w_o_t": np.ascontiguousarray(np.asarray(L1_gnn_W_O).T),
        "gate_logit": np.ascontiguousarray(L1_gnn_gate_logit).reshape(1, 1),
        "log_sigma": np.ascontiguousarray(L1_gnn_log_sigma).reshape(1, 1),
    }
    nc = bacc.Bacc("TRN2", target_bir_lowering=False, num_devices=1, dynamic_dma_scratch_size=1024)
    args = [nc.dram_tensor(f"{n}_dram", a.shape, mybir.dt.from_np(a.dtype), kind="ExternalInput").ap()
            for n, a in arrays.items()]
    out = nc.dram_tensor("out_dram", x.shape, mybir.dt.from_np(np.dtype("float32")), kind="ExternalOutput").ap()
    adjacency_two_layer_kernel(nc, *args, out)
    r = run_bass_kernel_spmd(nc, [{f"{n}_dram": a for n, a in arrays.items()}], core_ids=[0])
    return r.results[0]["out_dram"]
```

```python
import concourse.bass as bass
from concourse import mybir
from contextlib import ExitStack


def adjacency_two_layer_kernel(nc: bass.Bass, x, adj, adj_ext, bm, w_lang_t, w_grav_t, w_v, w_o_t,
                               gate_logit, log_sigma, out):
    fp32, fp32r = mybir.dt.float32, mybir.dt.float32r
    ALU = mybir.AluOpType
    ACT = mybir.ActivationFunctionType
    AX = mybir.AxisListType

    B, C, N = x.shape
    PAIRS = B // 2
    CB, NB = C // 128, N // 128
    LN_EPS, TINY = 1e-5, 1e-8
    SLOPE = 0.01
    CE = C + 2

    with ExitStack() as ctx:
        def sb(name, shape, dt=fp32):
            return ctx.enter_context(nc.sbuf_tensor(name, shape, dt))

        def sem(name):
            return ctx.enter_context(nc.semaphore(name))

        wl_hi, wl_lo = sb("wl_hi", [128, NB, N], fp32r), sb("wl_lo", [128, NB, N], fp32r)
        wg_hi, wg_lo = sb("wg_hi", [128, NB, N], fp32r), sb("wg_lo", [128, NB, N], fp32r)
        wov_hi, wov_lo = sb("wov_hi", [128, NB, N], fp32r), sb("wov_lo", [128, NB, N], fp32r)
        ae_hi, ae_lo = sb("ae_hi", [128, CB, CE], fp32r), sb("ae_lo", [128, CB, CE], fp32r)
        adjz = sb("adjz", [128, CB, C])
        bm_rows = sb("bm_rows", [128, C])
        ident = sb("ident", [128, 128])
        minus_half = sb("minus_half", [128, 2])
        gate = sb("gate", [128, 8])
        sig = sb("sig", [128, 8])
        x_in = sb("x_in", [128, 2, CB, N])
        h = sb("h", [128, CB, N])
        h_hi, h_lo = sb("h_hi", [128, CB, N], fp32r), sb("h_lo", [128, CB, N], fp32r)
        hab = sb("hab", [128, 2, C])
        ha_hi, ha_lo = sb("ha_hi", [128, NB, C], fp32r), sb("ha_lo", [128, NB, C], fp32r)
        v_row = sb("v_row", [128, N])
        p_f = sb("p_f", [128, NB, N])
        p_hi, p_lo = sb("p_hi", [128, NB, N], fp32r), sb("p_lo", [128, NB, N], fp32r)
        p_sum = sb("p_sum", [128, N])
        rz_row = sb("rz_row", [128, N])
        x1 = sb("x1", [128, 2, CB, N])
        keep = sb("keep", [128, 2, CB, N])
        h2 = sb("h2", [128, 2, CB, N])
        ht_hi, ht_lo = sb("ht_hi", [128, NB, 2 * C], fp32r), sb("ht_lo", [128, NB, 2 * C], fp32r)
        z_hi, z_lo = sb("z_hi", [128, NB, 2 * C], fp32r), sb("z_lo", [128, NB, 2 * C], fp32r)
        v_hi, v_lo = sb("v_hi", [128, 2 * CB, N], fp32r), sb("v_lo", [128, 2 * CB, N], fp32r)
        g_l = sb("g_l", [128, 2, CB, C])
        g_g = sb("g_g", [128, 2, CB, C])
        rows = sb("rows", [128, 2, 2, C])
        k_f = sb("k_f", [128, 2, CB, C])
        kt_hi, kt_lo = sb("kt_hi", [128, 2, CB, C], fp32r), sb("kt_lo", [128, 2, CB, C], fp32r)
        bn = sb("bn", [128, 4, CB, 6])
        mv = sb("mv", [128, 4, 5, CB])
        var = sb("var", [128, 4, CB])
        nmean = sb("nmean", [128, 4, CB])
        rstd = sb("rstd", [128, 4, CB])
        nmr = sb("nmr", [128, 4, CB])
        qk = sb("qk", [128, 2, NB, 2])
        q_top = sb("q_top", [128, 2])
        q_max = sb("q_max", [128, 2])
        q_less = sb("q_less", [128, 2, NB])
        k_pos = sb("k_pos", [128, 2, NB])
        col_a, col_b, col_v = sb("col_a", [128, 2, NB]), sb("col_b", [128, 2, NB]), sb("col_v", [128, 2, NB])
        z_sum, z_inv = sb("z_sum", [128, 2, NB]), sb("z_inv", [128, 2, NB])
        junk = sb("junk", [128, 128])
        sq_l, sq_g = sb("sq_l", [128, 2, CB]), sb("sq_g", [128, 2, CB])
        sq_lm = sb("sq_lm", [128, 2, CB])
        r_norm = sb("r_norm", [128, 2, CB])
        c_sq = sb("c_sq", [128, 2, CB])
        deg = sb("deg", [128, 2, 2, CB])
        deg2 = sb("deg2", [128, 2, 2, CB])
        deg3 = sb("deg3", [128, 2, 2, CB])
        deg_inv = sb("deg_inv", [128, 2, 2, CB])
        coef = sb("coef", [128, 2, 2, CB])

        bank = [ctx.enter_context(nc.psum_tensor(f"bank{j}", [128, 512], fp32)) for j in range(8)]
        ae_f = h2[:, 0, :, 0:CE]
        L0_BANK, SUM_BANK, L1_BANK = bank[0:2], bank[2:4], bank[4:8]

        HT_BANK = [L1_BANK[j] for j in (0, 1, 2, 3)]
        ZL_BANK = [L1_BANK[j] for j in (0, 1, 0, 1)]
        KT_BANK = [L1_BANK[j] for j in (2, 3)]
        V_BANK = [L1_BANK[j] for j in (2, 3, 0, 3)]
        GL_BANK = [L1_BANK[j] for j in (1, 2)]
        ZG_BANK = [L1_BANK[j] for j in (3, 0, 1, 2)]
        GG_BANK = [L1_BANK[j] for j in (0, 1)]
        ROW_BANK = [L1_BANK[j] for j in (2, 3)]

        s_const = sem("s_const")
        s_w = [sem(f"s_w{j}") for j in range(4)]
        s_xin = [sem("s_xin0"), sem("s_xin1")]
        s_stored = [sem("s_stored0"), sem("s_stored1")]
        s_ident, s_half, s_adjz = sem("s_ident"), sem("s_half"), sem("s_adjz")
        s_gate_act, s_gate = sem("s_gate_act"), sem("s_gate")
        s_chi, s_clo = sem("s_chi"), sem("s_clo")
        s_ae = sem("s_ae")
        s_wov = sem("s_wov")
        s_bn = [sem("s_bn_l0"), sem("s_bn_l1")]
        s_mv = [sem("s_mv_l0"), sem("s_mv_l1")]
        s_var = [sem("s_var_l0"), sem("s_var_l1")]
        s_rstd = [sem("s_rstd_l0"), sem("s_rstd_l1")]
        s_nmr = [sem("s_nmr_l0"), sem("s_nmr_l1")]
        s_h = sem("s_h")
        s_hhi = sem("s_hhi")
        s_hlo = sem("s_hlo")
        s_ha = sem("s_ha")
        s_hab = sem("s_hab")
        s_qk = sem("s_qk")
        s_hahi, s_halo = sem("s_hahi"), sem("s_halo")
        s_qtop = sem("s_qtop")
        s_qt = sem("s_qt")
        s_qmax = sem("s_qmax")
        s_arg = sem("s_arg")
        s_cols = sem("s_cols")
        s_vt = sem("s_vt")
        s_vrow = sem("s_vrow")
        s_pf = sem("s_pf")
        s_phi, s_plo = sem("s_phi"), sem("s_plo")
        s_part = sem("s_part")
        s_num = sem("s_num")
        s_tt = sem("s_tt")
        s_zsum = sem("s_zsum")
        s_zinv = sem("s_zinv")
        s_rzt = sem("s_rzt")
        s_rz = sem("s_rz")
        s_y = sem("s_y")
        s_x1 = sem("s_x1")
        s_h2 = sem("s_h2")
        s_keep = sem("s_keep")
        s_ht = sem("s_ht")
        s_hthi, s_htlo = sem("s_hthi"), sem("s_htlo")
        s_zl, s_zg = sem("s_zl"), sem("s_zg")
        s_zhi, s_zlo = sem("s_zhi"), sem("s_zlo")
        s_v = sem("s_v")
        s_vhi, s_vlo = sem("s_vhi"), sem("s_vlo")
        s_gl, s_gg = sem("s_gl"), sem("s_gg")
        s_glc, s_ggc = sem("s_glc"), sem("s_ggc")
        s_sql, s_sqg = sem("s_sql"), sem("s_sqg")
        s_sqlm = sem("s_sqlm")
        s_rn = sem("s_rn")
        s_bc = sem("s_bc")
        s_rows = sem("s_rows")
        s_mrn = sem("s_mrn")
        s_kl, s_kg = sem("s_kl"), sem("s_kg")
        s_dist = sem("s_dist")
        s_csq = sem("s_csq")
        s_exp = sem("s_exp")
        s_deg = sem("s_deg")
        s_coef = sem("s_coef")
        s_ks = sem("s_ks")
        s_k = sem("s_k")
        s_kt = sem("s_kt")
        s_kthi, s_ktlo = sem("s_kthi"), sem("s_ktlo")
        s_kv = sem("s_kv")
        s_out = sem("s_out")

        block = ctx.enter_context(nc.Block())

        def run(eng, step):
            step(-1, False, False, True, True)
            step(0, False, True, True, True)
            with eng.Fori(1, PAIRS - 2) as i:
                step(i, True, True, True, True)
            step(PAIRS - 2, True, True, True, False)
            step(PAIRS - 1, True, True, False, False)
            step(PAIRS, True, False, False, False)

        x_v = x.rearrange("b (t p) n -> b p t n", p=128)
        out_v = out.rearrange("b (t p) n -> b p t n", p=128)

        @block.sync
        def _(sp):
            def load(p, b):
                sp.dma_start(x_in[:, b], x_v[bass.ds(2 * p + b, 1)].rearrange("b p t n -> p (b t) n")
                             ).then_inc(s_xin[b], 16)

            def store(i, b):
                sp.wait_ge(s_out, 4 * i + 2 * b + 2)
                sp.dma_start(out_v[bass.ds(2 * i + b, 1)].rearrange("b p t n -> p (b t) n"), keep[:, b]
                             ).then_inc(s_stored[b], 16)

            load(0, 0)
            sp.dma_start(ae_f, adj_ext.rearrange("(t p) n -> p t n", p=128)).then_inc(s_const, 16)
            sp.dma_start(bm_rows[:], bm.rearrange("(a n) -> a n", a=1).to_broadcast([128, C])).then_inc(s_const, 16)
            sp.dma_start(adjz[:], adj.rearrange("(t p) n -> p t n", p=128)).then_inc(s_const, 16)
            sp.dma_start(gate[:, 0:1], gate_logit.to_broadcast([128, 1])).then_inc(s_const, 16)
            sp.dma_start(sig[:, 0:1], log_sigma.to_broadcast([128, 1])).then_inc(s_const, 16)
            load(0, 1)
            sp.dma_start(keep[:].rearrange("p b t n -> p (b t) n"),
                         w_v.rearrange("(t p) n -> p t n", p=128)).then_inc(s_w[0], 16)
            sp.dma_start(x1[:].rearrange("p b t n -> p (b t) n"),
                         w_o_t.rearrange("(t p) n -> p t n", p=128)).then_inc(s_w[1], 16)
            sp.dma_start(p_f[:], w_lang_t.rearrange("(t p) n -> p t n", p=128)).then_inc(s_w[2], 16)
            sp.wait_ge(s_clo, 1)
            sp.dma_start(keep[:].rearrange("p b t n -> p (b t) n"),
                         w_grav_t.rearrange("(t p) n -> p t n", p=128)).then_inc(s_w[3], 16)

            def step(i, late, l1, l0, ahead):
                p = i + 1
                for b in range(2):
                    if late:
                        store(i - 1, b)
                    if ahead:
                        sp.wait_ge(s_x1, 2 * p + b + 1)
                        load(p + 1, b)

            run(sp, step)
            sp.wait_ge(s_stored[0], 16 * PAIRS)
            sp.wait_ge(s_stored[1], 16 * PAIRS)

        @block.gpsimd
        def _(pool):
            pool.memset(minus_half[:], -0.5).then_inc(s_half, 1)
            pool.memset(ident[:], 0.0).then_inc(s_ident, 1)
            pool.wait_ge(s_ident, 1)
            pool.affine_select(out=ident[:], in_=ident[:], compare_op=ALU.not_equal, fill=1.0, base=0,
                               pattern=[[-1, 128]], channel_multiplier=1).then_inc(s_ident, 1)
            pool.wait_ge(s_const, 16 * 5)
            pool.affine_select(out=adjz[:], in_=adjz[:], compare_op=ALU.not_equal, fill=0.0, base=0,
                               pattern=[[128, CB], [-1, C]], channel_multiplier=1).then_inc(s_adjz, 1)
            pool.wait_ge(s_half, 1)

            def norm_scale(layer, p, b):
                n = 2 * p + b + 1
                j = 2 * layer + b
                pool.wait_ge(s_var[layer], n)
                pool.tensor_tensor(rstd[:, j], var[:, j], minus_half[:], ALU.pow).then_inc(s_rstd[layer], 1)
                pool.wait_ge(s_rstd[layer], n)
                pool.tensor_tensor(nmr[:, j], nmean[:, j], rstd[:, j], ALU.mult).then_inc(s_nmr[layer], 1)

            def h_low(p, b):
                pool.wait_ge(s_hhi, 2 * p + b + 1)
                pool.wait_ge(s_ha, 8 * p + 4 * b)
                pool.tensor_tensor(h_lo[:], h[:], h_hi[:].bitcast(fp32), ALU.subtract).then_inc(s_hlo, 1)

            def p_total(p, b):
                n = 6 * p + 3 * b
                pool.wait_ge(s_pf, 8 * p + 4 * b + 2)
                pool.wait_ge(s_tt, 2 * p + b)
                pool.tensor_tensor(p_sum[:], p_f[:, 0], p_f[:, 1], ALU.add).then_inc(s_part, 1)
                for j in range(2, NB):
                    pool.wait_ge(s_pf, 8 * p + 4 * b + j + 1)
                    pool.wait_ge(s_part, n + j - 1)
                    pool.tensor_tensor(p_sum[:], p_sum[:], p_f[:, j], ALU.add).then_inc(s_part, 1)

            def mask_scaled(i, b):
                pool.wait_ge(s_rows, 2 * i + b + 1)
                for t in range(CB):
                    last = pool.tensor_tensor(k_f[:, b, t], adjz[:, t], rows[:, b, 0], ALU.mult)
                last.then_inc(s_mrn, 1)

            def inverse_norm(i, b):
                pool.wait_ge(s_sqlm, 2 * i + b + 1)
                pool.tensor_tensor(r_norm[:, b], sq_lm[:, b], minus_half[:], ALU.pow).then_inc(s_rn, 1)

            def step(i, late, l1, l0, ahead):
                p = i + 1
                if late:
                    mask_scaled(i - 1, 0)
                    mask_scaled(i - 1, 1)
                if l0:
                    p_total(p, 0)
                    norm_scale(0, p, 1)
                    h_low(p, 1)
                    norm_scale(1, p, 0)
                    p_total(p, 1)
                if l1:
                    inverse_norm(i, 0)
                    inverse_norm(i, 1)
                if ahead:
                    norm_scale(0, p + 1, 0)
                    h_low(p + 1, 0)
                if l0:
                    norm_scale(1, p, 1)

            norm_scale(0, 0, 0)
            h_low(0, 0)
            run(pool, step)

        @block.scalar
        def _(act):
            def copy(o, i):
                return act.activation(o, i, ACT.Copy)

            act.wait_ge(s_const, 16 * 5)
            copy(ae_hi[:], ae_f).then_inc(s_ae, 1)
            act.activation(gate[:, 1:2], gate[:, 0:1], ACT.Exp, scale=-1.0).then_inc(s_gate_act, 1)
            act.activation(sig[:, 1:2], sig[:, 0:1], ACT.Exp).then_inc(s_gate_act, 1)

            def h_make(p, b):
                n = 2 * p + b
                act.wait_ge(s_xin[b], 16 * p + 16)
                act.wait_ge(s_nmr[0], n + 1)
                act.wait_ge(s_hlo, n)
                for t in range(CB):
                    last = act.activation(h[:, t], x_in[:, b, t], ACT.Relu, scale=rstd[:, b, t:t + 1],
                                          bias=nmr[:, b, t:t + 1])
                last.then_inc(s_h, 1)
                act.wait_ge(s_h, n + 1)
                act.wait_ge(s_ha, 8 * p + 4 * b)
                copy(h_hi[:], h[:]).then_inc(s_hhi, 1)

            def ha_high(p, b, j):
                act.wait_ge(s_num, 4 * p + 2 * b)
                act.wait_ge(s_hab, 8 * p + 4 * b + j + 1)
                copy(ha_hi[:, j], hab[:, j % 2]).then_inc(s_hahi, 1)

            def columns(p, b):
                act.wait_ge(s_arg, 2 * p + b + 1)
                act.activation(col_v[:, b], k_pos[:, b], ACT.Exp, scale=SLOPE - 1.0)
                act.activation(col_a[:, b], q_less[:, b], ACT.Exp)
                act.activation(col_b[:, b], q_less[:, b], ACT.Exp, scale=SLOPE).then_inc(s_cols, 1)

            def v_rows(p, b):
                act.wait_ge(s_vt, 2 * p + b + 1)
                act.wait_ge(s_pf, 8 * p + 4 * b)
                copy(v_row[:], L0_BANK[1][:]).then_inc(s_vrow, 1)

            def p_high(p, b, j):
                act.wait_ge(s_num, 4 * p + 2 * b)
                act.wait_ge(s_pf, 8 * p + 4 * b + j + 1)
                copy(p_hi[:, j], p_f[:, j]).then_inc(s_phi, 1)

            def rz_rows(p, b):
                act.wait_ge(s_rzt, 2 * p + b + 1)
                act.wait_ge(s_y, 4 * p + 2 * b)
                copy(rz_row[:], L0_BANK[1][:]).then_inc(s_rz, 1)

            def h2_make(p, b):
                act.wait_ge(s_nmr[1], 2 * p + b + 1)
                act.wait_ge(s_x1, 2 * p + b + 1)
                act.wait_ge(s_ht, 4 * p)
                for t in range(CB):
                    last = act.activation(h2[:, b, t], x1[:, b, t], ACT.Relu, scale=rstd[:, 2 + b, t:t + 1],
                                          bias=nmr[:, 2 + b, t:t + 1])
                last.then_inc(s_h2, 1)

            def ht_high(i, f):
                act.wait_ge(s_ht, 4 * i + f + 1)
                act.wait_ge(s_v, 4 * i)
                act.wait_ge(s_zg, 4 * i)
                copy(ht_hi[:, :, f * 128:(f + 1) * 128],
                     HT_BANK[f][:].rearrange("p (t n) -> p t n", t=NB)).then_inc(s_hthi, 1)

            def z_high(i, kind, e, s_z, psum):
                act.wait_ge(s_z, 4 * i + e + 1)
                if kind == 0:
                    act.wait_ge(s_gg, 2 * i)
                else:
                    act.wait_ge(s_gl, 2 * i + 2)
                copy(z_hi[:, e], psum[:]).then_inc(s_zhi, 1)

            def v_high(i, f, late):
                act.wait_ge(s_v, 4 * i + f + 1)
                if late:
                    act.wait_ge(s_kv, 4 * i - 2 + f // 2 * 2)
                copy(v_hi[:, f], V_BANK[f][:]).then_inc(s_vhi, 1)

            def gram_copy(i, b, g, psum, s_g, s_copied):
                act.wait_ge(s_g, 2 * i + b + 1)
                act.wait_ge(s_k, 4 * i)
                copy(g[:, b].rearrange("p t n -> p (t n)"), psum[:]).then_inc(s_copied, 1)

            def kt_high(i, b):
                act.wait_ge(s_kt, 2 * i + b + 1)
                act.wait_ge(s_kv, 4 * i)
                copy(kt_hi[:, b].rearrange("p t n -> p (t n)"), KT_BANK[b][:]).then_inc(s_kthi, 1)

            def row_copy(i, b):
                act.wait_ge(s_bc, 2 * i + b + 1)
                act.wait_ge(s_mrn, 2 * i)
                act.wait_ge(s_dist, 2 * i)
                copy(rows[:, b].rearrange("p t n -> p (t n)"), ROW_BANK[b][:]).then_inc(s_rows, 1)

            def exponentials(i, b):
                act.wait_ge(s_dist, 2 * i + b + 1)
                act.wait_ge(s_csq, 2 * i + b + 1)
                act.wait_ge(s_gate, 7)
                for t in range(CB):
                    act.activation(g_g[:, b, t], g_g[:, b, t], ACT.Exp, scale=sig[:, 4:5],
                                   bias=c_sq[:, b, t:t + 1]).then_inc(s_exp, 1)

            def k_scaled(i, b):
                act.wait_ge(s_coef, 2 * i + b + 1)
                for t in range(CB):
                    act.activation(k_f[:, b, t], k_f[:, b, t], ACT.Copy, scale=coef[:, b, 0, t:t + 1]
                                   ).then_inc(s_ks, 1)

            def keep_copy(i, b):
                act.wait_ge(s_x1, 2 * i + b + 1)
                act.wait_ge(s_stored[b], 16 * i)
                copy(keep[:, b], x1[:, b]).then_inc(s_keep, 1)

            def step(i, late, l1, l0, ahead):
                p = i + 1
                if late:
                    row_copy(i - 1, 0)
                if l0:
                    ha_high(p, 0, 0)
                if l1:
                    ht_high(i, 0)
                if late:
                    row_copy(i - 1, 1)
                if l0:
                    ha_high(p, 0, 1)
                if l1:
                    ht_high(i, 1)
                if l0:
                    ha_high(p, 0, 2)
                if l1:
                    ht_high(i, 2)
                    ht_high(i, 3)
                if l0:
                    ha_high(p, 0, 3)
                if late:
                    exponentials(i - 1, 0)
                if l0:
                    columns(p, 0)
                if l1:
                    z_high(i, 0, 0, s_zl, ZL_BANK[0])
                if late:
                    k_scaled(i - 1, 0)
                if l1:
                    z_high(i, 0, 1, s_zl, ZL_BANK[1])
                if late:
                    exponentials(i - 1, 1)
                if l0:
                    v_rows(p, 0)
                if l1:
                    z_high(i, 0, 2, s_zl, ZL_BANK[2])
                if late:
                    kt_high(i - 1, 0)
                if l0:
                    p_high(p, 0, 0)
                    p_high(p, 0, 1)
                if l1:
                    z_high(i, 0, 3, s_zl, ZL_BANK[3])
                if l0:
                    p_high(p, 0, 2)
                    p_high(p, 0, 3)
                if l1:
                    v_high(i, 0, late)
                if late:
                    k_scaled(i - 1, 1)
                if l1:
                    keep_copy(i, 0)
                if late:
                    kt_high(i - 1, 1)
                if l0:
                    h_make(p, 1)
                    rz_rows(p, 0)
                if l1:
                    v_high(i, 1, late)
                if l0:
                    ha_high(p, 1, 0)
                    ha_high(p, 1, 1)
                    ha_high(p, 1, 2)
                    ha_high(p, 1, 3)
                if l1:
                    v_high(i, 2, late)
                if l0:
                    columns(p, 1)
                if l1:
                    gram_copy(i, 0, g_l, GL_BANK[0], s_gl, s_glc)
                    gram_copy(i, 1, g_l, GL_BANK[1], s_gl, s_glc)
                if l0:
                    v_rows(p, 1)
                    p_high(p, 1, 0)
                if l1:
                    z_high(i, 1, 0, s_zg, ZG_BANK[0])
                if l0:
                    p_high(p, 1, 1)
                    h2_make(p, 0)
                    p_high(p, 1, 2)
                if l1:
                    keep_copy(i, 1)
                if l0:
                    p_high(p, 1, 3)
                if l1:
                    z_high(i, 1, 1, s_zg, ZG_BANK[1])
                if ahead:
                    h_make(p + 1, 0)
                if l1:
                    z_high(i, 1, 2, s_zg, ZG_BANK[2])
                    z_high(i, 1, 3, s_zg, ZG_BANK[3])
                if l0:
                    rz_rows(p, 1)
                if l1:
                    v_high(i, 3, late)
                    gram_copy(i, 0, g_g, GG_BANK[0], s_gg, s_ggc)
                    gram_copy(i, 1, g_g, GG_BANK[1], s_gg, s_ggc)
                if l0:
                    h2_make(p, 1)

            h_make(0, 0)
            act.wait_ge(s_w[0], 16)
            copy(z_hi[:], keep[:].rearrange("p b t n -> p (b t) n")).then_inc(s_chi, 1)
            act.wait_ge(s_w[1], 16)
            copy(v_hi[:], x1[:].rearrange("p b t n -> p (b t) n")).then_inc(s_chi, 1)
            act.wait_ge(s_w[2], 16)
            copy(wl_hi[:], p_f[:]).then_inc(s_chi, 1)
            act.wait_ge(s_w[3], 16)
            copy(wg_hi[:], keep[:].rearrange("p b t n -> p (b t) n")).then_inc(s_chi, 1)
            for d in range(NB):
                act.wait_ge(s_wov, d + 1)
                copy(wov_hi[:, d], L1_BANK[d][:]).then_inc(s_chi, 1)
            run(act, step)

        @block.tensor
        def _(pe):
            def three(o, a_hi, a_lo, b_hi, b_lo, first, last):
                pe.matmul(o, a_hi, b_hi, start=first, stop=False)
                pe.matmul(o, a_hi, b_lo, start=False, stop=False)
                return pe.matmul(o, a_lo, b_hi, start=False, stop=last)

            def column_to_row(o, col):
                return pe.transpose(o, col.to_broadcast([128, 128]), ident[:])

            def adj_h(p, b, j):
                if j == 0:
                    pe.wait_ge(s_hlo, 2 * p + b + 1)
                    pe.wait_ge(s_hhi, 2 * p + b + 1)
                if j == 0:
                    pe.wait_ge(s_zsum, 2 * p + b)
                elif j == 1:
                    pe.wait_ge(s_rz, 2 * p + b)
                else:
                    pe.wait_ge(s_hab, 8 * p + 4 * b + j - 1)
                    pe.wait_ge(s_qk, 8 * p + 4 * b + j - 1)
                for t in range(CB):
                    m = slice(j * 128, (j + 1) * 128)
                    mm = three(L0_BANK[j % 2][:, 0:CE], h_hi[:, t, m], h_lo[:, t, m],
                               ae_hi[:, t], ae_lo[:, t], t == 0, t == CB - 1)
                mm.then_inc(s_ha, 1)

            def q_row(p, b):
                pe.wait_ge(s_qtop, 2 * p + b + 1)
                column_to_row(L0_BANK[0][:, 0:128], q_top[:, b:b + 1]).then_inc(s_qt, 1)

            def v_to_row(p, b):
                pe.wait_ge(s_cols, 2 * p + b + 1)
                for j in range(NB):
                    mm = column_to_row(L0_BANK[1][:, j * 128:(j + 1) * 128], col_v[:, b, j:j + 1])
                mm.then_inc(s_vt, 1)

            def attend(i, p, b, o, late):
                if late:
                    pe.wait_ge(s_out, 4 * i - 2 + 2 * b)
                elif b:
                    pe.wait_ge(s_y, 4 * p + 2)
                for j in range(NB):
                    if o == 0:
                        pe.wait_ge(s_phi, 8 * p + 4 * b + j + 1)
                        pe.wait_ge(s_plo, 8 * p + 4 * b + j + 1)
                        pe.wait_ge(s_halo, 8 * p + 4 * b + j + 1)
                    m = slice(o * 128, (o + 1) * 128)
                    mm = three(SUM_BANK[o][:], ha_hi[:, j, m], ha_lo[:, j, m],
                               p_hi[:, j], p_lo[:, j], j == 0, j == NB - 1)
                mm.then_inc(s_num, 1)

            def total(p, b):
                pe.wait_ge(s_part, 6 * p + 3 * b + 3)
                pe.wait_ge(s_qmax, 2 * p + b + 1)
                for j in range(NB):
                    mm = pe.transpose(L0_BANK[0][:, j * 128:(j + 1) * 128], p_sum[:, j * 128:(j + 1) * 128], ident[:])
                mm.then_inc(s_tt, 1)

            def rz_to_row(p, b):
                pe.wait_ge(s_zinv, 2 * p + b + 1)
                pe.wait_ge(s_vrow, 2 * p + b + 1)
                for j in range(NB):
                    mm = column_to_row(L0_BANK[1][:, j * 128:(j + 1) * 128], z_inv[:, b, j:j + 1])
                mm.then_inc(s_rzt, 1)

            def h2_transpose(i, f):
                b, t = divmod(f, CB)
                pe.wait_ge(s_h2, 2 * i + b + 1)
                pe.wait_ge(s_ggc if f < 2 else s_rows, 2 * i)
                for d in range(NB):
                    mm = pe.transpose(HT_BANK[f][:, d * 128:(d + 1) * 128],
                                      h2[:, b, t, d * 128:(d + 1) * 128], ident[:])
                mm.then_inc(s_ht, 1)

            def z_block(e, hi, lo, psum, s_z):
                m = slice(e * 128, (e + 1) * 128)
                for d in range(NB):
                    mm = three(psum[:], hi[:, d, m], lo[:, d, m], ht_hi[:, d], ht_lo[:, d], d == 0, d == NB - 1)
                mm.then_inc(s_z, 1)

            def v_block(f):
                m = slice(f * 128, (f + 1) * 128)
                for d in range(NB):
                    mm = three(V_BANK[f][:], ht_hi[:, d, m], ht_lo[:, d, m], wov_hi[:, d], wov_lo[:, d],
                               d == 0, d == NB - 1)
                mm.then_inc(s_v, 1)

            def gram(b, psum, s_g):
                for t in range(CB):
                    o = psum[:, t * C:(t + 1) * C]
                    m = slice(b * C + t * 128, b * C + (t + 1) * 128)
                    n = slice(b * C, (b + 1) * C)
                    for e in range(NB):
                        mm = three(o, z_hi[:, e, m], z_lo[:, e, m], z_hi[:, e, n], z_lo[:, e, n],
                                   e == 0, e == NB - 1)
                mm.then_inc(s_g, 1)

            def rows_of(i, b):
                pe.wait_ge(s_rn, 2 * i + b + 1)
                pe.wait_ge(s_sqg, 4 * i + 2 * b + 2)
                pe.wait_ge(s_vlo, 4 * i + 4)
                for t in range(CB):
                    column_to_row(ROW_BANK[b][:, t * 128:(t + 1) * 128], r_norm[:, b, t:t + 1])
                    mm = column_to_row(ROW_BANK[b][:, C + t * 128:C + (t + 1) * 128], sq_g[:, b, t:t + 1])
                mm.then_inc(s_bc, 1)

            def k_transpose(i, b):
                pe.wait_ge(s_k, 4 * i + 2 * b + 2)
                for mb in range(CB):
                    for t in range(CB):
                        mm = pe.transpose(KT_BANK[b][:, mb * C + t * 128:mb * C + (t + 1) * 128],
                                          k_f[:, b, t, mb * 128:(mb + 1) * 128], ident[:])
                mm.then_inc(s_kt, 1)

            def mix(i, b, y):
                pe.wait_ge(s_y, y)
                pe.wait_ge(s_ktlo, 2 * i + b + 1)
                pe.wait_ge(s_vlo, 4 * i + 4)
                for t in range(CB):
                    for mb in range(CB):
                        n = slice(t * 128, (t + 1) * 128)
                        mm = three(SUM_BANK[t][:], kt_hi[:, b, mb, n], kt_lo[:, b, mb, n],
                                   v_hi[:, 2 * b + mb], v_lo[:, 2 * b + mb], mb == 0, mb == CB - 1)
                    mm.then_inc(s_kv, 1)

            def step(i, late, l1, l0, ahead):
                p = i + 1
                if l0:
                    adj_h(p, 0, 0)
                    adj_h(p, 0, 1)
                if late:
                    rows_of(i - 1, 0)
                if l1:
                    h2_transpose(i, 0)
                    h2_transpose(i, 1)
                if late:
                    rows_of(i - 1, 1)
                if l0:
                    adj_h(p, 0, 2)
                if l1:
                    h2_transpose(i, 2)
                    h2_transpose(i, 3)
                if l0:
                    adj_h(p, 0, 3)
                    q_row(p, 0)
                if l1:
                    pe.wait_ge(s_htlo, 4 * i + 4)
                    z_block(0, wl_hi, wl_lo, ZL_BANK[0], s_zl)
                    z_block(1, wl_hi, wl_lo, ZL_BANK[1], s_zl)
                    pe.wait_ge(s_zlo, 8 * i + 1)
                    z_block(2, wl_hi, wl_lo, ZL_BANK[2], s_zl)
                if l0:
                    v_to_row(p, 0)
                if late:
                    k_transpose(i - 1, 0)
                if l1:
                    pe.wait_ge(s_zlo, 8 * i + 2)
                    z_block(3, wl_hi, wl_lo, ZL_BANK[3], s_zl)
                if late:
                    mix(i - 1, 0, 4 * i + 4 if l1 else 4 * PAIRS)
                if l1:
                    if late:
                        pe.wait_ge(s_ktlo, 2 * i - 1)
                    v_block(0)
                if l0:
                    attend(i, p, 0, 0, late)
                    attend(i, p, 0, 1, late)
                    total(p, 0)
                if late:
                    k_transpose(i - 1, 1)
                if l1:
                    if late:
                        pe.wait_ge(s_ktlo, 2 * i)
                    v_block(1)
                if l0:
                    rz_to_row(p, 0)
                    adj_h(p, 1, 0)
                    adj_h(p, 1, 1)
                    adj_h(p, 1, 2)
                if late:
                    if not l0:
                        pe.wait_ge(s_out, 4 * i - 2)
                    mix(i - 1, 1, 4 * p + 2 if l0 else 4 * PAIRS)
                if l0:
                    adj_h(p, 1, 3)
                if l1:
                    pe.wait_ge(s_zlo, 8 * i + 3)
                    v_block(2)
                if l0:
                    q_row(p, 1)
                if l1:
                    pe.wait_ge(s_zlo, 8 * i + 4)
                    gram(0, GL_BANK[0], s_gl)
                if l0:
                    v_to_row(p, 1)
                if l1:
                    pe.wait_ge(s_vlo, 4 * i + 1)
                    gram(1, GL_BANK[1], s_gl)
                    pe.wait_ge(s_vlo, 4 * i + 2)
                    z_block(0, wg_hi, wg_lo, ZG_BANK[0], s_zg)
                    pe.wait_ge(s_vlo, 4 * i + 3)
                    z_block(1, wg_hi, wg_lo, ZG_BANK[1], s_zg)
                    pe.wait_ge(s_glc, 2 * i + 1)
                    z_block(2, wg_hi, wg_lo, ZG_BANK[2], s_zg)
                if l0:
                    attend(i, p, 1, 0, late)
                    attend(i, p, 1, 1, late)
                    total(p, 1)
                if l1:
                    pe.wait_ge(s_glc, 2 * i + 2)
                    z_block(3, wg_hi, wg_lo, ZG_BANK[3], s_zg)
                if l0:
                    rz_to_row(p, 1)
                if l1:
                    pe.wait_ge(s_zlo, 8 * i + 5)
                    v_block(3)
                    pe.wait_ge(s_zlo, 8 * i + 8)
                    gram(0, GG_BANK[0], s_gg)
                    gram(1, GG_BANK[1], s_gg)

            pe.wait_ge(s_ident, 2)
            pe.wait_ge(s_ae, 2)
            pe.wait_ge(s_chi, 2)
            pe.wait_ge(s_clo, 2)
            for d in range(NB):
                m = slice(d * 128, (d + 1) * 128)
                for k in range(NB):
                    mm = three(L1_BANK[d][:], z_hi[:, k, m], z_lo[:, k, m], v_hi[:, k], v_lo[:, k],
                               k == 0, k == NB - 1)
                mm.then_inc(s_wov, 1)
            run(pe, step)

        @block.vector
        def _(dve):
            def minus_hi(o, f, hi):
                return dve.tensor_tensor(o, f, hi.bitcast(fp32), ALU.subtract)

            def stats(layer, src, p, b):
                n, j = 2 * p + b, 2 * layer + b
                if layer == 0:
                    dve.wait_ge(s_xin[b], 16 * p + 16)
                    if not isinstance(p, int) or p > 0:
                        dve.wait_ge(s_h, 2 * p + b - 1)
                else:
                    dve.wait_ge(s_x1, n + 1)
                    dve.wait_ge(s_h2, 2 * p)
                for t in range(CB):
                    dve.bn_stats(bn[:, j, t], src[:, b, t]).then_inc(s_bn[layer], 1)
                dve.wait_ge(s_bn[layer], 2 * n + 2)
                dve.tensor_tensor(mv[:, j, 0], bn[:, j, :, 1], bn[:, j, :, 4], ALU.add)
                dve.tensor_tensor(mv[:, j, 1], bn[:, j, :, 1], bn[:, j, :, 4], ALU.subtract)
                dve.tensor_tensor(mv[:, j, 2], bn[:, j, :, 2], bn[:, j, :, 5], ALU.add).then_inc(s_mv[layer], 1)
                dve.wait_ge(s_mv[layer], 2 * n + 1)
                dve.tensor_scalar(nmean[:, j], mv[:, j, 0], -0.5, None, ALU.mult)
                dve.scalar_tensor_tensor(out=mv[:, j, 3], in0=mv[:, j, 1], scalar=0.25, in1=mv[:, j, 1],
                                         op0=ALU.mult, op1=ALU.mult)
                dve.tensor_scalar(mv[:, j, 4], mv[:, j, 2], 1.0 / N, LN_EPS, ALU.mult, ALU.add
                                  ).then_inc(s_mv[layer], 1)
                dve.wait_ge(s_mv[layer], 2 * n + 2)
                dve.tensor_tensor(var[:, j], mv[:, j, 3], mv[:, j, 4], ALU.add).then_inc(s_var[layer], 1)

            def ha_take(p, b, j):
                n = 8 * p + 4 * b + j + 1
                dve.wait_ge(s_ha, n)
                if j >= 2:
                    dve.wait_ge(s_halo, n - 2)
                dve.tensor_tensor(hab[:, j % 2], L0_BANK[j % 2][:, 0:C], bm_rows[:], ALU.add).then_inc(s_hab, 1)
                dve.tensor_copy(qk[:, b, j], L0_BANK[j % 2][:, C:CE]).then_inc(s_qk, 1)

            def ha_low(p, b, j):
                dve.wait_ge(s_hahi, 8 * p + 4 * b + j + 1)
                minus_hi(ha_lo[:, j], hab[:, j % 2], ha_hi[:, j]).then_inc(s_halo, 1)

            def q_tops(p, b):
                dve.wait_ge(s_qk, 8 * p + 4 * b + 4)
                dve.tensor_reduce(q_top[:, b:b + 1], qk[:, b, :, 0], AX.X, ALU.max).then_inc(s_qtop, 1)

            def arguments(p, b):
                n = 2 * p + b + 1
                dve.wait_ge(s_qt, n)
                dve.tensor_reduce(q_max[:, b:b + 1], L0_BANK[0][:, 0:128], AX.X, ALU.max).then_inc(s_qmax, 1)
                dve.wait_ge(s_qmax, n)
                dve.tensor_scalar(q_less[:, b], qk[:, b, :, 0], q_max[:, b:b + 1], None, ALU.subtract)
                dve.tensor_scalar(k_pos[:, b], qk[:, b, :, 1], q_max[:, b:b + 1], 0.0, ALU.add, ALU.max
                                  ).then_inc(s_arg, 1)

            def p_make(p, b, j):
                if j == 0:
                    dve.wait_ge(s_vrow, 2 * p + b + 1)
                    dve.wait_ge(s_phi, 8 * p + 4 * b)
                    dve.wait_ge(s_plo, 8 * p + 4 * b)
                    dve.wait_ge(s_part, 6 * p + 3 * b)
                dve.tensor_scalar(p_f[:, j], v_row[:], col_b[:, b, j:j + 1], col_a[:, b, j:j + 1],
                                  ALU.mult, ALU.max).then_inc(s_pf, 1)

            def p_low(p, b, j):
                dve.wait_ge(s_num, 4 * p + 2 * b)
                dve.wait_ge(s_phi, 8 * p + 4 * b + j + 1)
                minus_hi(p_lo[:, j], p_f[:, j], p_hi[:, j]).then_inc(s_plo, 1)

            def z_column(p, b):
                n = 2 * p + b + 1
                dve.wait_ge(s_tt, n)
                dve.tensor_reduce(z_sum[:, b], L0_BANK[0][:].rearrange("p (t n) -> p t n", t=NB), AX.X, ALU.add
                                  ).then_inc(s_zsum, 1)
                dve.wait_ge(s_zsum, n)
                dve.reciprocal(z_inv[:, b], z_sum[:, b]).then_inc(s_zinv, 1)

            def relu_over_z(p, b, o, l1):
                n = 2 * p + b
                dve.wait_ge(s_rz, n + 1)
                if l1:
                    dve.wait_ge(s_keep, n - 1)
                dve.wait_ge(s_num, 2 * n + o + 1)
                dve.scalar_tensor_tensor(out=x1[:, b, o], in0=SUM_BANK[o][:], scalar=0.0, in1=rz_row[:],
                                         op0=ALU.max, op1=ALU.mult).then_inc(s_y, 1)

            def residual(p, b):
                n = 2 * p + b
                dve.wait_ge(s_y, 2 * n + 2)
                dve.tensor_tensor(x1[:, b], x1[:, b], x_in[:, b], ALU.add).then_inc(s_x1, 1)

            def ht_low(i, f):
                dve.wait_ge(s_hthi, 4 * i + f + 1)
                m = slice(f * 128, (f + 1) * 128)
                minus_hi(ht_lo[:, :, m], HT_BANK[f][:].rearrange("p (t n) -> p t n", t=NB),
                         ht_hi[:, :, m]).then_inc(s_htlo, 1)

            def z_low(i, kind, e, psum):
                dve.wait_ge(s_zhi, 8 * i + 4 * kind + e + 1)
                minus_hi(z_lo[:, e], psum[:], z_hi[:, e]).then_inc(s_zlo, 1)

            def v_low(i, f):
                dve.wait_ge(s_vhi, 4 * i + f + 1)
                minus_hi(v_lo[:, f], V_BANK[f][:], v_hi[:, f]).then_inc(s_vlo, 1)

            def diagonal(i, b, g, s_copied, sq, s_sq, first):
                dve.wait_ge(s_copied, 2 * i + b + 1)
                for t in range(CB):
                    n = 4 * i + 2 * b + t
                    dve.wait_ge(s_sq, n)
                    if first is not None and b == 0 and t == 0:
                        dve.wait_ge(*first)
                    dve.scalar_tensor_tensor(out=junk[:], in0=g[:, b, t, t * 128:(t + 1) * 128], scalar=1.0,
                                             in1=ident[:], op0=ALU.mult, op1=ALU.mult,
                                             accum_out=sq[:, b, t:t + 1]).then_inc(s_sq, 1)

            def guard(i, b):
                dve.wait_ge(s_sql, 4 * i + 2 * b + 2)
                dve.tensor_scalar(sq_lm[:, b], sq_l[:, b], TINY * TINY, None, ALU.max).then_inc(s_sqlm, 1)

            def kernels_raw(i, b):
                dve.wait_ge(s_mrn, 2 * i + b + 1)
                for t in range(CB):
                    dve.scalar_tensor_tensor(out=k_f[:, b, t], in0=g_l[:, b, t], scalar=0.0, in1=k_f[:, b, t],
                                             op0=ALU.max, op1=ALU.mult,
                                             accum_out=deg[:, b, 0, t:t + 1]).then_inc(s_kl, 1)

            def distances(i, b):
                dve.wait_ge(s_rows, 2 * i + b + 1)
                dve.wait_ge(s_sqg, 4 * i + 2 * b + 2)
                for t in range(CB):
                    last = dve.scalar_tensor_tensor(out=g_g[:, b, t], in0=g_g[:, b, t], scalar=-2.0,
                                                    in1=rows[:, b, 1], op0=ALU.mult, op1=ALU.add)
                last.then_inc(s_dist, 1)
                dve.tensor_scalar(c_sq[:, b], sq_g[:, b], sig[:, 4:5], None, ALU.mult).then_inc(s_csq, 1)

            def kernels_masked(i, b):
                n = 4 * i + 2 * b
                for t in range(CB):
                    dve.wait_ge(s_exp, n + t + 1)
                    dve.scalar_tensor_tensor(out=g_g[:, b, t], in0=g_g[:, b, t], scalar=1.0, in1=adjz[:, t],
                                             op0=ALU.min, op1=ALU.mult,
                                             accum_out=deg[:, b, 1, t:t + 1]).then_inc(s_kg, 1)

            def coefficients(i, b):
                n = 4 * i + 2 * b
                dve.wait_ge(s_kl, n + 2)
                dve.wait_ge(s_kg, n + 2)
                dve.tensor_tensor(deg2[:, b, 0], deg[:, b, 0], r_norm[:, b], ALU.mult)
                dve.tensor_copy(deg2[:, b, 1], deg[:, b, 1]).then_inc(s_deg, 1)
                dve.wait_ge(s_deg, 6 * i + 3 * b + 1)
                dve.tensor_scalar(deg3[:, b], deg2[:, b], TINY, None, ALU.max).then_inc(s_deg, 1)
                dve.wait_ge(s_deg, 6 * i + 3 * b + 2)
                dve.reciprocal(deg_inv[:, b], deg3[:, b]).then_inc(s_deg, 1)
                dve.wait_ge(s_deg, 6 * i + 3 * b + 3)
                dve.scalar_tensor_tensor(out=coef[:, b, 0], in0=deg_inv[:, b, 0], scalar=gate[:, 3:4],
                                         in1=r_norm[:, b], op0=ALU.mult, op1=ALU.mult)
                dve.tensor_scalar(coef[:, b, 1], deg_inv[:, b, 1], gate[:, 4:5], None, ALU.mult
                                  ).then_inc(s_coef, 1)

            def k_sum(i, b):
                n = 4 * i + 2 * b
                for t in range(CB):
                    dve.wait_ge(s_ks, n + t + 1)
                    dve.scalar_tensor_tensor(out=k_f[:, b, t], in0=g_g[:, b, t], scalar=coef[:, b, 1, t:t + 1],
                                             in1=k_f[:, b, t], op0=ALU.mult, op1=ALU.add).then_inc(s_k, 1)

            def kt_low(i, b):
                dve.wait_ge(s_kthi, 2 * i + b + 1)
                minus_hi(kt_lo[:, b].rearrange("p t n -> p (t n)"), KT_BANK[b][:],
                         kt_hi[:, b].rearrange("p t n -> p (t n)")).then_inc(s_ktlo, 1)

            def output(i, b):
                dve.wait_ge(s_keep, 2 * i + b + 1)
                for t in range(CB):
                    dve.wait_ge(s_kv, 4 * i + 2 * b + t + 1)
                    dve.tensor_tensor(keep[:, b, t], SUM_BANK[t][:], keep[:, b, t], ALU.add).then_inc(s_out, 1)

            def step(i, late, l1, l0, ahead):
                p = i + 1
                if l0:
                    ha_take(p, 0, 0)
                    ha_take(p, 0, 1)
                    ha_low(p, 0, 0)
                    ha_take(p, 0, 2)
                    ha_low(p, 0, 1)
                if l1:
                    ht_low(i, 0)
                if l0:
                    ha_low(p, 0, 2)
                if l1:
                    ht_low(i, 1)
                    ht_low(i, 2)
                    ht_low(i, 3)
                if l0:
                    ha_take(p, 0, 3)
                    q_tops(p, 0)
                if late:
                    distances(i - 1, 0)
                    kernels_raw(i - 1, 0)
                if l0:
                    ha_low(p, 0, 3)
                if late:
                    kernels_masked(i - 1, 0)
                if l0:
                    arguments(p, 0)
                if late:
                    distances(i - 1, 1)
                    coefficients(i - 1, 0)
                if l1:
                    z_low(i, 0, 0, ZL_BANK[0])
                if late:
                    k_sum(i - 1, 0)
                    kernels_raw(i - 1, 1)
                if l1:
                    z_low(i, 0, 1, ZL_BANK[1])
                if l0:
                    p_make(p, 0, 0)
                    p_make(p, 0, 1)
                if late:
                    kt_low(i - 1, 0)
                if l0:
                    p_make(p, 0, 2)
                    p_make(p, 0, 3)
                    p_low(p, 0, 0)
                if late:
                    kernels_masked(i - 1, 1)
                if l0:
                    p_low(p, 0, 1)
                if late:
                    output(i - 1, 0)
                if l0:
                    p_low(p, 0, 2)
                if l1:
                    z_low(i, 0, 2, ZL_BANK[2])
                if l0:
                    p_low(p, 0, 3)
                if l1:
                    z_low(i, 0, 3, ZL_BANK[3])
                if l0:
                    stats(0, x_in, p, 1)
                if late:
                    coefficients(i - 1, 1)
                    k_sum(i - 1, 1)
                    kt_low(i - 1, 1)
                if l1:
                    v_low(i, 0)
                if l0:
                    z_column(p, 0)
                    relu_over_z(p, 0, 0, l1)
                    relu_over_z(p, 0, 1, l1)
                    ha_take(p, 1, 0)
                    ha_take(p, 1, 1)
                    ha_low(p, 1, 0)
                    residual(p, 0)
                    ha_take(p, 1, 2)
                if l1:
                    v_low(i, 1)
                if l0:
                    ha_low(p, 1, 1)
                    ha_take(p, 1, 3)
                    ha_low(p, 1, 2)
                    ha_low(p, 1, 3)
                    q_tops(p, 1)
                    arguments(p, 1)
                if l1:
                    diagonal(i, 0, g_l, s_glc, sq_l, s_sql, (s_sqg, 4 * i))
                    v_low(i, 2)
                if l0:
                    stats(1, x1, p, 0)
                if l1:
                    diagonal(i, 1, g_l, s_glc, sq_l, s_sql, None)
                if late:
                    output(i - 1, 1)
                if l1:
                    guard(i, 0)
                if l0:
                    p_make(p, 1, 0)
                    p_make(p, 1, 1)
                    p_low(p, 1, 0)
                    p_make(p, 1, 2)
                    p_low(p, 1, 1)
                if l1:
                    z_low(i, 1, 0, ZG_BANK[0])
                if l0:
                    p_make(p, 1, 3)
                if l1:
                    guard(i, 1)
                if l0:
                    p_low(p, 1, 2)
                    p_low(p, 1, 3)
                if ahead:
                    stats(0, x_in, p + 1, 0)
                if l1:
                    z_low(i, 1, 1, ZG_BANK[1])
                if l0:
                    z_column(p, 1)
                if l1:
                    z_low(i, 1, 2, ZG_BANK[2])
                if l0:
                    relu_over_z(p, 1, 0, l1)
                if l1:
                    z_low(i, 1, 3, ZG_BANK[3])
                if l0:
                    relu_over_z(p, 1, 1, l1)
                if l1:
                    v_low(i, 3)
                if l0:
                    residual(p, 1)
                    stats(1, x1, p, 1)
                if l1:
                    diagonal(i, 0, g_g, s_ggc, sq_g, s_sqg, (s_sql, 4 * i + 4))
                    diagonal(i, 1, g_g, s_ggc, sq_g, s_sqg, None)

            stats(0, x_in, 0, 0)
            dve.wait_ge(s_ae, 1)
            minus_hi(ae_lo[:], ae_f, ae_hi[:]).then_inc(s_ae, 1)
            dve.wait_ge(s_gate_act, 2)
            dve.tensor_scalar(gate[:, 2:3], gate[:, 1:2], 1.0, None, ALU.add).then_inc(s_gate, 1)
            dve.tensor_scalar(sig[:, 2:3], sig[:, 1:2], sig[:, 1:2], 2.0, ALU.mult, ALU.mult).then_inc(s_gate, 1)
            dve.wait_ge(s_gate, 2)
            dve.reciprocal(gate[:, 3:4], gate[:, 2:3]).then_inc(s_gate, 1)
            dve.reciprocal(sig[:, 3:4], sig[:, 2:3]).then_inc(s_gate, 1)
            dve.wait_ge(s_gate, 4)
            dve.tensor_scalar(gate[:, 4:5], gate[:, 3:4], -1.0, 1.0, ALU.mult, ALU.add).then_inc(s_gate, 1)
            dve.tensor_scalar(sig[:, 4:5], sig[:, 3:4], -1.0, None, ALU.mult).then_inc(s_gate, 1)
            dve.wait_ge(s_gate, 6)
            dve.wait_ge(s_adjz, 1)
            dve.tensor_copy(gate[:, 5:6], gate[:, 4:5]).then_inc(s_gate, 1)
            dve.wait_ge(s_chi, 1)
            minus_hi(z_lo[:], keep[:].rearrange("p b t n -> p (b t) n"), z_hi[:]).then_inc(s_clo, 1)
            dve.wait_ge(s_chi, 2)
            minus_hi(v_lo[:], x1[:].rearrange("p b t n -> p (b t) n"), v_hi[:]).then_inc(s_clo, 1)
            dve.wait_ge(s_chi, 3)
            minus_hi(wl_lo[:], p_f[:], wl_hi[:]).then_inc(s_clo, 1)
            dve.wait_ge(s_chi, 4)
            minus_hi(wg_lo[:], keep[:].rearrange("p b t n -> p (b t) n"), wg_hi[:]).then_inc(s_clo, 1)
            for d in range(NB):
                dve.wait_ge(s_chi, 5 + d)
                minus_hi(wov_lo[:, d], L1_BANK[d][:], wov_hi[:, d]).then_inc(s_clo, 1)
            run(dve, step)


def kernel(x, adj, L0_gnn_wq, L0_gnn_wk, L0_gnn_bm, L1_gnn_W_lang, L1_gnn_W_grav, L1_gnn_W_V, L1_gnn_W_O,
           L1_gnn_gate_logit, L1_gnn_log_sigma):
    import numpy as np
    import concourse.bacc as bacc
    from concourse.bass_utils import run_bass_kernel_spmd

    arrays = {
        "x": np.ascontiguousarray(x),
        "adj": np.ascontiguousarray(adj),
        "adj_ext": np.concatenate([np.asarray(adj).T, np.asarray(L0_gnn_wq)[:, None],
                                   np.asarray(L0_gnn_wk)[:, None]], axis=1),
        "bm": np.ascontiguousarray(L0_gnn_bm),
        "w_lang_t": np.ascontiguousarray(np.asarray(L1_gnn_W_lang).T),
        "w_grav_t": np.ascontiguousarray(np.asarray(L1_gnn_W_grav).T),
        "w_v": np.ascontiguousarray(L1_gnn_W_V),
        "w_o_t": np.ascontiguousarray(np.asarray(L1_gnn_W_O).T),
        "gate_logit": np.ascontiguousarray(L1_gnn_gate_logit).reshape(1, 1),
        "log_sigma": np.ascontiguousarray(L1_gnn_log_sigma).reshape(1, 1),
    }
    nc = bacc.Bacc("TRN2", target_bir_lowering=False, num_devices=1, dynamic_dma_scratch_size=1024)
    args = [nc.dram_tensor(f"{n}_dram", a.shape, mybir.dt.from_np(a.dtype), kind="ExternalInput").ap()
            for n, a in arrays.items()]
    out = nc.dram_tensor("out_dram", x.shape, mybir.dt.from_np(np.dtype("float32")), kind="ExternalOutput").ap()
    adjacency_two_layer_kernel(nc, *args, out)
    r = run_bass_kernel_spmd(nc, [{f"{n}_dram": a for n, a in arrays.items()}], core_ids=[0])
    return r.results[0]["out_dram"]
```

```python
import concourse.bass as bass
from concourse import mybir
from contextlib import ExitStack


def adjacency_two_layer_kernel(nc: bass.Bass, x, adj, adj_ext, bm, w_lang_t, w_grav_t, w_v, w_o_t,
                               gate_logit, log_sigma, out):
    fp32, fp32r = mybir.dt.float32, mybir.dt.float32r
    ALU = mybir.AluOpType
    ACT = mybir.ActivationFunctionType
    AX = mybir.AxisListType

    B, C, N = x.shape
    PAIRS = B // 2
    CB, NB = C // 128, N // 128
    LN_EPS, TINY = 1e-5, 1e-8
    SLOPE = 0.01
    CE = C + 2

    with ExitStack() as ctx:
        def sb(name, shape, dt=fp32):
            return ctx.enter_context(nc.sbuf_tensor(name, shape, dt))

        def sem(name):
            return ctx.enter_context(nc.semaphore(name))

        wl_hi, wl_lo = sb("wl_hi", [128, NB, N], fp32r), sb("wl_lo", [128, NB, N], fp32r)
        wg_hi, wg_lo = sb("wg_hi", [128, NB, N], fp32r), sb("wg_lo", [128, NB, N], fp32r)
        wov_hi, wov_lo = sb("wov_hi", [128, NB, N], fp32r), sb("wov_lo", [128, NB, N], fp32r)
        ae_hi, ae_lo = sb("ae_hi", [128, CB, CE], fp32r), sb("ae_lo", [128, CB, CE], fp32r)
        adjz = sb("adjz", [128, CB, C])
        bm_rows = sb("bm_rows", [128, C])
        ident = sb("ident", [128, 128])
        ones = sb("ones", [128, 2])
        minus_half = sb("minus_half", [128, 2])
        gate = sb("gate", [128, 8])
        sig = sb("sig", [128, 8])
        x_in = sb("x_in", [128, 2, CB, N])
        h = sb("h", [128, CB, N])
        h_hi, h_lo = sb("h_hi", [128, CB, N], fp32r), sb("h_lo", [128, CB, N], fp32r)
        hab = sb("hab", [128, 2, C])
        ha_hi, ha_lo = sb("ha_hi", [128, NB, C], fp32r), sb("ha_lo", [128, NB, C], fp32r)
        v_row = sb("v_row", [128, N])
        p_f = sb("p_f", [128, NB, N])
        p_hi, p_lo = sb("p_hi", [128, NB, N], fp32r), sb("p_lo", [128, NB, N], fp32r)
        p_sum = sb("p_sum", [128, N])
        rz_row = sb("rz_row", [128, N])
        x1 = sb("x1", [128, 2, CB, N])
        keep = sb("keep", [128, 2, CB, N])
        h2 = sb("h2", [128, 2, CB, N])
        ht_hi, ht_lo = sb("ht_hi", [128, NB, 2 * C], fp32r), sb("ht_lo", [128, NB, 2 * C], fp32r)
        z_hi, z_lo = sb("z_hi", [128, NB, 2 * C], fp32r), sb("z_lo", [128, NB, 2 * C], fp32r)
        v_hi, v_lo = sb("v_hi", [128, 2 * CB, N], fp32r), sb("v_lo", [128, 2 * CB, N], fp32r)
        g_l = sb("g_l", [128, 2, CB, C])
        g_g = sb("g_g", [128, 2, CB, C])
        rows = sb("rows", [128, 2, 2, C])
        k_f = sb("k_f", [128, 2, CB, C])
        kt_hi, kt_lo = sb("kt_hi", [128, 2, CB, C], fp32r), sb("kt_lo", [128, 2, CB, C], fp32r)
        bn = sb("bn", [128, 4, CB, 6])
        mv = sb("mv", [128, 4, 5, CB])
        var = sb("var", [128, 4, CB])
        nmean = sb("nmean", [128, 4, CB])
        rstd = sb("rstd", [128, 4, CB])
        nmr = sb("nmr", [128, 4, CB])
        qk = sb("qk", [128, 2, NB, 2])
        q_top = sb("q_top", [128, 2])
        q_max = sb("q_max", [128, 2])
        q_less = sb("q_less", [128, 2, NB])
        k_pos = sb("k_pos", [128, 2, NB])
        col_a, col_b, col_v = sb("col_a", [128, 2, NB]), sb("col_b", [128, 2, NB]), sb("col_v", [128, 2, NB])
        z_inv = sb("z_inv", [128, 2, NB])
        junk = sb("junk", [128, 128])
        sq_l, sq_g = sb("sq_l", [128, 2, CB]), sb("sq_g", [128, 2, CB])
        sq_lm = sb("sq_lm", [128, 2, CB])
        r_norm = sb("r_norm", [128, 2, CB])
        c_sq = sb("c_sq", [128, 2, CB])
        deg = sb("deg", [128, 2, 2, CB])
        deg2 = sb("deg2", [128, 2, 2, CB])
        deg3 = sb("deg3", [128, 2, 2, CB])
        deg_inv = sb("deg_inv", [128, 2, 2, CB])
        coef = sb("coef", [128, 2, 2, CB])

        bank = [ctx.enter_context(nc.psum_tensor(f"bank{j}", [128, 512], fp32)) for j in range(8)]
        ae_f = h2[:, 0, :, 0:CE]
        L0_BANK, SUM_BANK, L1_BANK = bank[0:2], bank[2:4], bank[4:8]

        HT_BANK = [L1_BANK[j] for j in (0, 1, 2, 3)]
        ZL_BANK = [L1_BANK[j] for j in (0, 1, 0, 1)]
        KT_BANK = [L1_BANK[j] for j in (2, 3)]
        V_BANK = [L1_BANK[j] for j in (2, 3, 0, 3)]
        GL_BANK = [L1_BANK[j] for j in (1, 2)]
        ZG_BANK = [L1_BANK[j] for j in (3, 0, 1, 2)]
        GG_BANK = [L1_BANK[j] for j in (0, 1)]
        ROW_BANK = [L1_BANK[j] for j in (2, 3)]

        s_const = sem("s_const")
        s_w = [sem(f"s_w{j}") for j in range(4)]
        s_xin = [sem("s_xin0"), sem("s_xin1")]
        s_stored = [sem("s_stored0"), sem("s_stored1")]
        s_ident, s_half, s_adjz = sem("s_ident"), sem("s_half"), sem("s_adjz")
        s_gate_act, s_gate = sem("s_gate_act"), sem("s_gate")
        s_chi, s_clo = sem("s_chi"), sem("s_clo")
        s_wlo = sem("s_wlo")
        s_ovhi, s_ovlo = sem("s_ovhi"), sem("s_ovlo")
        s_ae = sem("s_ae")
        s_wov = sem("s_wov")
        s_bn = [sem("s_bn_l0"), sem("s_bn_l1")]
        s_mv = [sem("s_mv_l0"), sem("s_mv_l1")]
        s_var = [sem("s_var_l0"), sem("s_var_l1")]
        s_rstd = [sem("s_rstd_l0"), sem("s_rstd_l1")]
        s_nmr = [sem("s_nmr_l0"), sem("s_nmr_l1")]
        s_h = sem("s_h")
        s_hhi = sem("s_hhi")
        s_hlo = [sem("s_hlo0"), sem("s_hlo1")]
        s_ha = sem("s_ha")
        s_hab = sem("s_hab")
        s_qk = sem("s_qk")
        s_hahi, s_halo = sem("s_hahi"), sem("s_halo")
        s_qtop = sem("s_qtop")
        s_qt = sem("s_qt")
        s_qmax = sem("s_qmax")
        s_arg = sem("s_arg")
        s_cols = sem("s_cols")
        s_vt = sem("s_vt")
        s_vrow = sem("s_vrow")
        s_pf = sem("s_pf")
        s_phi, s_plo = sem("s_phi"), sem("s_plo")
        s_part = sem("s_part")
        s_num = sem("s_num")
        s_tt = sem("s_tt")
        s_zinv = sem("s_zinv")
        s_rzt = sem("s_rzt")
        s_rz = sem("s_rz")
        s_y = sem("s_y")
        s_x1 = sem("s_x1")
        s_h2 = sem("s_h2")
        s_keep = sem("s_keep")
        s_ht = sem("s_ht")
        s_hthi, s_htlo = sem("s_hthi"), sem("s_htlo")
        s_zl, s_zg = sem("s_zl"), sem("s_zg")
        s_zhi, s_zlo = sem("s_zhi"), sem("s_zlo")
        s_v = sem("s_v")
        s_vhi, s_vlo = sem("s_vhi"), sem("s_vlo")
        s_gl, s_gg = sem("s_gl"), sem("s_gg")
        s_glc, s_ggc = sem("s_glc"), sem("s_ggc")
        s_sql, s_sqg = sem("s_sql"), sem("s_sqg")
        s_sqlm = sem("s_sqlm")
        s_rn = sem("s_rn")
        s_bc = sem("s_bc")
        s_rows = sem("s_rows")
        s_mrn = sem("s_mrn")
        s_kl, s_kg = sem("s_kl"), sem("s_kg")
        s_dist = sem("s_dist")
        s_csq = sem("s_csq")
        s_exp = sem("s_exp")
        s_deg = sem("s_deg")
        s_coef = sem("s_coef")
        s_ks = sem("s_ks")
        s_k = sem("s_k")
        s_kt = sem("s_kt")
        s_kthi, s_ktlo = sem("s_kthi"), sem("s_ktlo")
        s_kv = sem("s_kv")
        s_out = sem("s_out")

        block = ctx.enter_context(nc.Block())

        def run(eng, start, step, finish):
            start()
            step(0, False, True, True)
            with eng.Fori(1, PAIRS - 2) as i:
                step(i, True, True, True)
            step(PAIRS - 2, True, True, False)
            step(PAIRS - 1, True, False, False)
            finish()

        x_v = x.rearrange("b (t p) n -> b p t n", p=128)
        out_v = out.rearrange("b (t p) n -> b p t n", p=128)

        @block.sync
        def _(sp):
            def load(p, b):
                sp.dma_start(x_in[:, b], x_v[bass.ds(2 * p + b, 1)].rearrange("b p t n -> p (b t) n")
                             ).then_inc(s_xin[b], 16)

            def store(i, b):
                sp.wait_ge(s_out, 4 * i + 2 * b + 2)
                sp.dma_start(out_v[bass.ds(2 * i + b, 1)].rearrange("b p t n -> p (b t) n"), keep[:, b]
                             ).then_inc(s_stored[b], 16)

            load(0, 0)
            sp.dma_start(ae_f, adj_ext.rearrange("(t p) n -> p t n", p=128)).then_inc(s_const, 16)
            sp.dma_start(bm_rows[:], bm.rearrange("(a n) -> a n", a=1).to_broadcast([128, C])).then_inc(s_const, 16)
            sp.dma_start(adjz[:], adj.rearrange("(t p) n -> p t n", p=128)).then_inc(s_const, 16)
            sp.dma_start(gate[:, 0:1], gate_logit.to_broadcast([128, 1])).then_inc(s_const, 16)
            sp.dma_start(sig[:, 0:1], log_sigma.to_broadcast([128, 1])).then_inc(s_const, 16)
            load(0, 1)
            sp.dma_start(keep[:].rearrange("p b t n -> p (b t) n"),
                         w_v.rearrange("(t p) n -> p t n", p=128)).then_inc(s_w[0], 16)
            sp.dma_start(x1[:].rearrange("p b t n -> p (b t) n"),
                         w_o_t.rearrange("(t p) n -> p t n", p=128)).then_inc(s_w[1], 16)
            sp.dma_start(p_f[:], w_lang_t.rearrange("(t p) n -> p t n", p=128)).then_inc(s_w[2], 16)
            sp.wait_ge(s_clo, 1)
            sp.dma_start(keep[:].rearrange("p b t n -> p (b t) n"),
                         w_grav_t.rearrange("(t p) n -> p t n", p=128)).then_inc(s_w[3], 16)

            def start():
                for b in range(2):
                    sp.wait_ge(s_x1, b + 1)
                    load(1, b)

            def step(i, late, l0, ahead):
                p = i + 1
                for b in range(2):
                    if late:
                        store(i - 1, b)
                    if ahead:
                        sp.wait_ge(s_x1, 2 * p + b + 1)
                        load(p + 1, b)

            def finish():
                store(PAIRS - 1, 0)
                store(PAIRS - 1, 1)

            run(sp, start, step, finish)
            sp.wait_ge(s_stored[0], 16 * PAIRS)
            sp.wait_ge(s_stored[1], 16 * PAIRS)

        @block.gpsimd
        def _(pool):
            pool.memset(ones[:], 1.0).then_inc(s_half, 1)
            pool.memset(minus_half[:], -0.5).then_inc(s_half, 1)
            pool.memset(ident[:], 0.0).then_inc(s_ident, 1)
            pool.wait_ge(s_ident, 1)
            pool.affine_select(out=ident[:], in_=ident[:], compare_op=ALU.not_equal, fill=1.0, base=0,
                               pattern=[[-1, 128]], channel_multiplier=1).then_inc(s_ident, 1)
            pool.wait_ge(s_half, 2)

            def norm_scale(layer, p, b):
                n = 2 * p + b + 1
                j = 2 * layer + b
                pool.wait_ge(s_var[layer], n)
                pool.tensor_tensor(rstd[:, j], var[:, j], minus_half[:], ALU.pow).then_inc(s_rstd[layer], 1)
                pool.wait_ge(s_rstd[layer], n)
                pool.tensor_tensor(nmr[:, j], nmean[:, j], rstd[:, j], ALU.mult).then_inc(s_nmr[layer], 1)

            def weight_low(k):
                pool.wait_ge(s_chi, k + 1)
                src = p_f[:] if k == 2 else keep[:].rearrange("p b t n -> p (b t) n")
                hi, lo = ((wl_hi, wl_lo), (wg_hi, wg_lo))[k - 2]
                pool.tensor_tensor(lo[:], src, hi[:].bitcast(fp32), ALU.subtract).then_inc(s_wlo, 1)

            def h_low(p, b):
                pool.wait_ge(s_hhi, 4 * p + 2 * b + 1)
                pool.wait_ge(s_ha, 8 * p + 4 * b)
                pool.tensor_tensor(h_lo[:, 0], h[:, 0], h_hi[:, 0].bitcast(fp32), ALU.subtract).then_inc(s_hlo[0], 1)

            def p_total(p, b):
                n = 6 * p + 3 * b
                pool.wait_ge(s_pf, 8 * p + 4 * b + 2)
                pool.wait_ge(s_tt, 2 * p + b)
                pool.tensor_tensor(p_sum[:], p_f[:, 0], p_f[:, 1], ALU.add).then_inc(s_part, 1)
                for j in range(2, NB):
                    pool.wait_ge(s_pf, 8 * p + 4 * b + j + 1)
                    pool.wait_ge(s_part, n + j - 1)
                    pool.tensor_tensor(p_sum[:], p_sum[:], p_f[:, j], ALU.add).then_inc(s_part, 1)

            def mask_scaled(i, b):
                pool.wait_ge(s_rows, 2 * i + b + 1)
                for t in range(CB):
                    last = pool.tensor_tensor(k_f[:, b, t], adjz[:, t], rows[:, b, 0], ALU.mult)
                last.then_inc(s_mrn, 1)

            def inverse_norm(i, b):
                pool.wait_ge(s_sqlm, 2 * i + b + 1)
                pool.tensor_tensor(r_norm[:, b], sq_lm[:, b], minus_half[:], ALU.pow).then_inc(s_rn, 1)

            def start():
                weight_low(2)
                norm_scale(0, 0, 1)
                weight_low(3)
                p_total(0, 0)
                h_low(0, 1)
                norm_scale(0, 1, 0)
                norm_scale(1, 0, 0)
                p_total(0, 1)
                h_low(1, 0)
                norm_scale(1, 0, 1)

            def step(i, late, l0, ahead):
                p = i + 1
                if late:
                    mask_scaled(i - 1, 0)
                    mask_scaled(i - 1, 1)
                if l0:
                    p_total(p, 0)
                    norm_scale(0, p, 1)
                    h_low(p, 1)
                    norm_scale(1, p, 0)
                    p_total(p, 1)
                if ahead:
                    norm_scale(0, p + 1, 0)
                inverse_norm(i, 0)
                if ahead:
                    h_low(p + 1, 0)
                if l0:
                    norm_scale(1, p, 1)
                inverse_norm(i, 1)

            def finish():
                mask_scaled(PAIRS - 1, 0)
                mask_scaled(PAIRS - 1, 1)

            norm_scale(0, 0, 0)
            pool.wait_ge(s_const, 16 * 5)
            pool.affine_select(out=adjz[:], in_=adjz[:], compare_op=ALU.not_equal, fill=0.0, base=0,
                               pattern=[[128, CB], [-1, C]], channel_multiplier=1).then_inc(s_adjz, 1)
            h_low(0, 0)
            run(pool, start, step, finish)

        @block.scalar
        def _(act):
            def copy(o, i):
                return act.activation(o, i, ACT.Copy)

            act.wait_ge(s_const, 16 * 5)
            copy(ae_hi[:], ae_f).then_inc(s_ae, 1)
            act.activation(gate[:, 1:2], gate[:, 0:1], ACT.Exp, scale=-1.0).then_inc(s_gate_act, 1)
            act.activation(sig[:, 1:2], sig[:, 0:1], ACT.Exp).then_inc(s_gate_act, 1)

            def h_make(p, b):
                n = 2 * p + b
                act.wait_ge(s_xin[b], 16 * p + 16)
                act.wait_ge(s_nmr[0], n + 1)
                act.wait_ge(s_hlo[0], n)
                act.wait_ge(s_hlo[1], n)
                for t in range(CB):
                    last = act.activation(h[:, t], x_in[:, b, t], ACT.Relu, scale=rstd[:, b, t:t + 1],
                                          bias=nmr[:, b, t:t + 1])
                last.then_inc(s_h, 1)
                act.wait_ge(s_h, n + 1)
                act.wait_ge(s_ha, 8 * p + 4 * b)
                for t in range(CB):
                    copy(h_hi[:, t], h[:, t]).then_inc(s_hhi, 1)

            def ha_high(p, b, j):
                act.wait_ge(s_num, 4 * p + 2 * b)
                act.wait_ge(s_hab, 8 * p + 4 * b + j + 1)
                copy(ha_hi[:, j], hab[:, j % 2]).then_inc(s_hahi, 1)

            def columns(p, b):
                act.wait_ge(s_arg, 2 * p + b + 1)
                act.activation(col_v[:, b], k_pos[:, b], ACT.Exp, scale=SLOPE - 1.0)
                act.activation(col_a[:, b], q_less[:, b], ACT.Exp)
                act.activation(col_b[:, b], q_less[:, b], ACT.Exp, scale=SLOPE).then_inc(s_cols, 1)

            def v_rows(p, b):
                act.wait_ge(s_vt, 2 * p + b + 1)
                act.wait_ge(s_pf, 8 * p + 4 * b)
                copy(v_row[:], L0_BANK[1][:]).then_inc(s_vrow, 1)

            def p_high(p, b, j):
                act.wait_ge(s_num, 4 * p + 2 * b)
                act.wait_ge(s_pf, 8 * p + 4 * b + j + 1)
                copy(p_hi[:, j], p_f[:, j]).then_inc(s_phi, 1)

            def rz_rows(p, b):
                act.wait_ge(s_rzt, 2 * p + b + 1)
                act.wait_ge(s_y, 4 * p + 2 * b)
                copy(rz_row[:], L0_BANK[1][:]).then_inc(s_rz, 1)

            def h2_make(p, b):
                act.wait_ge(s_nmr[1], 2 * p + b + 1)
                act.wait_ge(s_x1, 2 * p + b + 1)
                act.wait_ge(s_ht, 4 * p)
                for t in range(CB):
                    last = act.activation(h2[:, b, t], x1[:, b, t], ACT.Relu, scale=rstd[:, 2 + b, t:t + 1],
                                          bias=nmr[:, 2 + b, t:t + 1])
                last.then_inc(s_h2, 1)

            def ht_high(i, f):
                act.wait_ge(s_ht, 4 * i + f + 1)
                act.wait_ge(s_v, 4 * i)
                act.wait_ge(s_zg, 4 * i)
                copy(ht_hi[:, :, f * 128:(f + 1) * 128],
                     HT_BANK[f][:].rearrange("p (t n) -> p t n", t=NB)).then_inc(s_hthi, 1)

            def z_high(i, kind, e, s_z, psum):
                act.wait_ge(s_z, 4 * i + e + 1)
                if kind == 0:
                    act.wait_ge(s_gg, 2 * i)
                else:
                    act.wait_ge(s_gl, 2 * i + 2)
                copy(z_hi[:, e], psum[:]).then_inc(s_zhi, 1)

            def v_high(i, f, late):
                act.wait_ge(s_v, 4 * i + f + 1)
                if late:
                    act.wait_ge(s_kv, 4 * i - 2 + f // 2 * 2)
                copy(v_hi[:, f], V_BANK[f][:]).then_inc(s_vhi, 1)

            def gram_copy(i, b, g, psum, s_g, s_copied):
                act.wait_ge(s_g, 2 * i + b + 1)
                act.wait_ge(s_k, 4 * i)
                copy(g[:, b].rearrange("p t n -> p (t n)"), psum[:]).then_inc(s_copied, 1)

            def kt_high(i, b):
                act.wait_ge(s_kt, 2 * i + b + 1)
                act.wait_ge(s_kv, 4 * i)
                copy(kt_hi[:, b].rearrange("p t n -> p (t n)"), KT_BANK[b][:]).then_inc(s_kthi, 1)

            def row_copy(i, b):
                act.wait_ge(s_bc, 2 * i + b + 1)
                act.wait_ge(s_mrn, 2 * i)
                act.wait_ge(s_dist, 2 * i)
                copy(rows[:, b].rearrange("p t n -> p (t n)"), ROW_BANK[b][:]).then_inc(s_rows, 1)

            def exponentials(i, b):
                act.wait_ge(s_dist, 2 * i + b + 1)
                act.wait_ge(s_csq, 2 * i + b + 1)
                act.wait_ge(s_gate, 7)
                for t in range(CB):
                    act.activation(g_g[:, b, t], g_g[:, b, t], ACT.Exp, scale=sig[:, 4:5],
                                   bias=c_sq[:, b, t:t + 1]).then_inc(s_exp, 1)

            def k_scaled(i, b):
                act.wait_ge(s_coef, 2 * i + b + 1)
                for t in range(CB):
                    act.activation(k_f[:, b, t], k_f[:, b, t], ACT.Copy, scale=coef[:, b, 0, t:t + 1]
                                   ).then_inc(s_ks, 1)

            def keep_copy(i, b):
                act.wait_ge(s_x1, 2 * i + b + 1)
                act.wait_ge(s_stored[b], 16 * i)
                copy(keep[:, b], x1[:, b]).then_inc(s_keep, 1)

            def weight_high(k):
                src = (keep, x1, p_f, keep)[k][:]
                act.wait_ge(s_w[k], 16)
                copy((z_hi, v_hi, wl_hi, wg_hi)[k][:], src if k == 2 else src.rearrange("p b t n -> p (b t) n")
                     ).then_inc(s_chi, 1)

            def wov_high(d):
                act.wait_ge(s_wov, d + 1)
                copy(wov_hi[:, d], L1_BANK[d][:]).then_inc(s_ovhi, 1)

            def start():
                weight_high(0)
                weight_high(1)
                ha_high(0, 0, 0)
                weight_high(2)
                ha_high(0, 0, 1)
                ha_high(0, 0, 2)
                weight_high(3)
                columns(0, 0)
                ha_high(0, 0, 3)
                v_rows(0, 0)
                p_high(0, 0, 0)
                p_high(0, 0, 1)
                p_high(0, 0, 2)
                p_high(0, 0, 3)
                h_make(0, 1)
                wov_high(0)
                rz_rows(0, 0)
                ha_high(0, 1, 0)
                wov_high(1)
                wov_high(2)
                ha_high(0, 1, 1)
                wov_high(3)
                ha_high(0, 1, 2)
                columns(0, 1)
                v_rows(0, 1)
                ha_high(0, 1, 3)
                p_high(0, 1, 0)
                p_high(0, 1, 1)
                p_high(0, 1, 2)
                p_high(0, 1, 3)
                h_make(1, 0)
                h2_make(0, 0)
                rz_rows(0, 1)
                h2_make(0, 1)
                act.wait_ge(s_wlo, 2)

            def step(i, late, l0, ahead):
                p = i + 1
                if late:
                    row_copy(i - 1, 0)
                ht_high(i, 0)
                if l0:
                    ha_high(p, 0, 0)
                if late:
                    row_copy(i - 1, 1)
                ht_high(i, 1)
                ht_high(i, 2)
                ht_high(i, 3)
                if l0:
                    ha_high(p, 0, 1)
                    ha_high(p, 0, 2)
                if late:
                    exponentials(i - 1, 0)
                if l0:
                    ha_high(p, 0, 3)
                z_high(i, 0, 0, s_zl, ZL_BANK[0])
                if l0:
                    columns(p, 0)
                if late:
                    k_scaled(i - 1, 0)
                z_high(i, 0, 1, s_zl, ZL_BANK[1])
                z_high(i, 0, 2, s_zl, ZL_BANK[2])
                if late:
                    kt_high(i - 1, 0)
                if l0:
                    v_rows(p, 0)
                if late:
                    exponentials(i - 1, 1)
                if l0:
                    p_high(p, 0, 0)
                    p_high(p, 0, 1)
                z_high(i, 0, 3, s_zl, ZL_BANK[3])
                if l0:
                    p_high(p, 0, 2)
                    p_high(p, 0, 3)
                if late:
                    k_scaled(i - 1, 1)
                    kt_high(i - 1, 1)
                if l0:
                    h_make(p, 1)
                    rz_rows(p, 0)
                keep_copy(i, 0)
                v_high(i, 0, late)
                if l0:
                    ha_high(p, 1, 0)
                    ha_high(p, 1, 1)
                v_high(i, 1, late)
                if l0:
                    ha_high(p, 1, 2)
                    columns(p, 1)
                    ha_high(p, 1, 3)
                v_high(i, 2, late)
                gram_copy(i, 0, g_l, GL_BANK[0], s_gl, s_glc)
                if l0:
                    v_rows(p, 1)
                gram_copy(i, 1, g_l, GL_BANK[1], s_gl, s_glc)
                if l0:
                    p_high(p, 1, 0)
                    p_high(p, 1, 1)
                keep_copy(i, 1)
                if l0:
                    p_high(p, 1, 2)
                z_high(i, 1, 0, s_zg, ZG_BANK[0])
                if l0:
                    p_high(p, 1, 3)
                z_high(i, 1, 1, s_zg, ZG_BANK[1])
                if l0:
                    h2_make(p, 0)
                z_high(i, 1, 2, s_zg, ZG_BANK[2])
                if ahead:
                    h_make(p + 1, 0)
                z_high(i, 1, 3, s_zg, ZG_BANK[3])
                if l0:
                    rz_rows(p, 1)
                gram_copy(i, 0, g_g, GG_BANK[0], s_gg, s_ggc)
                v_high(i, 3, late)
                if l0:
                    h2_make(p, 1)
                gram_copy(i, 1, g_g, GG_BANK[1], s_gg, s_ggc)

            def finish():
                row_copy(PAIRS - 1, 0)
                row_copy(PAIRS - 1, 1)
                exponentials(PAIRS - 1, 0)
                exponentials(PAIRS - 1, 1)
                k_scaled(PAIRS - 1, 0)
                kt_high(PAIRS - 1, 0)
                k_scaled(PAIRS - 1, 1)
                kt_high(PAIRS - 1, 1)

            h_make(0, 0)
            run(act, start, step, finish)

        @block.tensor
        def _(pe):
            def three(o, a_hi, a_lo, b_hi, b_lo, first, last):
                pe.matmul(o, a_hi, b_hi, start=first, stop=False)
                pe.matmul(o, a_hi, b_lo, start=False, stop=False)
                return pe.matmul(o, a_lo, b_hi, start=False, stop=last)

            def column_to_row(o, col):
                return pe.transpose(o, col.to_broadcast([128, 128]), ident[:])

            def adj_h(p, b, j):
                if j == 0:
                    pe.wait_ge(s_hlo[0], 2 * p + b + 1)
                    pe.wait_ge(s_hlo[1], 2 * p + b + 1)
                    pe.wait_ge(s_hhi, 4 * p + 2 * b + 2)
                if j == 0:
                    pe.wait_ge(s_zinv, 2 * p + b)
                elif j == 1:
                    pe.wait_ge(s_rz, 2 * p + b)
                else:
                    pe.wait_ge(s_hab, 8 * p + 4 * b + j - 1)
                    pe.wait_ge(s_qk, 8 * p + 4 * b + j - 1)
                for t in range(CB):
                    m = slice(j * 128, (j + 1) * 128)
                    mm = three(L0_BANK[j % 2][:, 0:CE], h_hi[:, t, m], h_lo[:, t, m],
                               ae_hi[:, t], ae_lo[:, t], t == 0, t == CB - 1)
                mm.then_inc(s_ha, 1)

            def q_row(p, b):
                pe.wait_ge(s_qtop, 2 * p + b + 1)
                column_to_row(L0_BANK[0][:, 0:128], q_top[:, b:b + 1]).then_inc(s_qt, 1)

            def v_to_row(p, b):
                pe.wait_ge(s_cols, 2 * p + b + 1)
                for j in range(NB):
                    mm = column_to_row(L0_BANK[1][:, j * 128:(j + 1) * 128], col_v[:, b, j:j + 1])
                mm.then_inc(s_vt, 1)

            def attend(i, p, b, o, late):
                if late:
                    pe.wait_ge(s_out, 4 * i - 2 + 2 * b)
                elif b:
                    pe.wait_ge(s_y, 4 * p + 2)
                for j in range(NB):
                    if o == 0:
                        pe.wait_ge(s_phi, 8 * p + 4 * b + j + 1)
                        pe.wait_ge(s_plo, 8 * p + 4 * b + j + 1)
                        pe.wait_ge(s_halo, 8 * p + 4 * b + j + 1)
                    m = slice(o * 128, (o + 1) * 128)
                    mm = three(SUM_BANK[o][:], ha_hi[:, j, m], ha_lo[:, j, m],
                               p_hi[:, j], p_lo[:, j], j == 0, j == NB - 1)
                mm.then_inc(s_num, 1)

            def total(p, b):
                pe.wait_ge(s_part, 6 * p + 3 * b + 3)
                pe.wait_ge(s_qmax, 2 * p + b + 1)
                for j in range(NB):
                    mm = pe.matmul(L0_BANK[0][:, 2 * j:2 * j + 2], p_sum[:, j * 128:(j + 1) * 128], ones[:],
                                   start=True, stop=True)
                mm.then_inc(s_tt, 1)

            def rz_to_row(p, b):
                pe.wait_ge(s_zinv, 2 * p + b + 1)
                pe.wait_ge(s_vrow, 2 * p + b + 1)
                for j in range(NB):
                    mm = column_to_row(L0_BANK[1][:, j * 128:(j + 1) * 128], z_inv[:, b, j:j + 1])
                mm.then_inc(s_rzt, 1)

            def h2_transpose(i, f):
                b, t = divmod(f, CB)
                pe.wait_ge(s_h2, 2 * i + b + 1)
                pe.wait_ge(s_ggc if f < 2 else s_rows, 2 * i)
                for d in range(NB):
                    mm = pe.transpose(HT_BANK[f][:, d * 128:(d + 1) * 128],
                                      h2[:, b, t, d * 128:(d + 1) * 128], ident[:])
                mm.then_inc(s_ht, 1)

            def z_block(e, hi, lo, psum, s_z):
                m = slice(e * 128, (e + 1) * 128)
                for d in range(NB):
                    mm = three(psum[:], hi[:, d, m], lo[:, d, m], ht_hi[:, d], ht_lo[:, d], d == 0, d == NB - 1)
                mm.then_inc(s_z, 1)

            def z_lang(i, e):
                if e == 0:
                    pe.wait_ge(s_htlo, 4 * i + 4)
                if e >= 2:
                    pe.wait_ge(s_zlo, 8 * i + e - 1)
                z_block(e, wl_hi, wl_lo, ZL_BANK[e], s_zl)

            def z_grav(i, e):
                pe.wait_ge(*((s_vlo, 4 * i + 2), (s_vlo, 4 * i + 3), (s_glc, 2 * i + 1), (s_glc, 2 * i + 2))[e])
                z_block(e, wg_hi, wg_lo, ZG_BANK[e], s_zg)

            def v_block(i, f, late):
                if f >= 2:
                    pe.wait_ge(s_zlo, 8 * i + (3, 5)[f - 2])
                elif late:
                    pe.wait_ge(s_ktlo, 2 * i - 1 + f)
                m = slice(f * 128, (f + 1) * 128)
                for d in range(NB):
                    mm = three(V_BANK[f][:], ht_hi[:, d, m], ht_lo[:, d, m], wov_hi[:, d], wov_lo[:, d],
                               d == 0, d == NB - 1)
                mm.then_inc(s_v, 1)

            def gram(b, psum, s_g):
                for t in range(CB):
                    o = psum[:, t * C:(t + 1) * C]
                    m = slice(b * C + t * 128, b * C + (t + 1) * 128)
                    n = slice(b * C, (b + 1) * C)
                    for e in range(NB):
                        mm = three(o, z_hi[:, e, m], z_lo[:, e, m], z_hi[:, e, n], z_lo[:, e, n],
                                   e == 0, e == NB - 1)
                mm.then_inc(s_g, 1)

            def gram_lang(i, b):
                if b == 0:
                    pe.wait_ge(s_zlo, 8 * i + 4)
                else:
                    pe.wait_ge(s_vlo, 4 * i + 1)
                gram(b, GL_BANK[b], s_gl)

            def gram_grav(i, b):
                if b == 0:
                    pe.wait_ge(s_zlo, 8 * i + 8)
                gram(b, GG_BANK[b], s_gg)

            def rows_of(i, b):
                pe.wait_ge(s_rn, 2 * i + b + 1)
                pe.wait_ge(s_sqg, 4 * i + 2 * b + 2)
                pe.wait_ge(s_vlo, 4 * i + 4)
                for t in range(CB):
                    column_to_row(ROW_BANK[b][:, t * 128:(t + 1) * 128], r_norm[:, b, t:t + 1])
                    mm = column_to_row(ROW_BANK[b][:, C + t * 128:C + (t + 1) * 128], sq_g[:, b, t:t + 1])
                mm.then_inc(s_bc, 1)

            def k_transpose(i, b):
                pe.wait_ge(s_k, 4 * i + 2 * b + 2)
                for mb in range(CB):
                    for t in range(CB):
                        mm = pe.transpose(KT_BANK[b][:, mb * C + t * 128:mb * C + (t + 1) * 128],
                                          k_f[:, b, t, mb * 128:(mb + 1) * 128], ident[:])
                mm.then_inc(s_kt, 1)

            def mix(i, b, y, l0):
                pe.wait_ge(s_y, y)
                if b and not l0:
                    pe.wait_ge(s_out, 4 * i + 2)
                pe.wait_ge(s_ktlo, 2 * i + b + 1)
                pe.wait_ge(s_vlo, 4 * i + 4)
                for t in range(CB):
                    for mb in range(CB):
                        n = slice(t * 128, (t + 1) * 128)
                        mm = three(SUM_BANK[t][:], kt_hi[:, b, mb, n], kt_lo[:, b, mb, n],
                                   v_hi[:, 2 * b + mb], v_lo[:, 2 * b + mb], mb == 0, mb == CB - 1)
                    mm.then_inc(s_kv, 1)

            def wov_block(d):
                pe.wait_ge(s_chi, 2)
                pe.wait_ge(s_clo, 2)
                m = slice(d * 128, (d + 1) * 128)
                for k in range(NB):
                    mm = three(L1_BANK[d][:], z_hi[:, k, m], z_lo[:, k, m], v_hi[:, k], v_lo[:, k],
                               k == 0, k == NB - 1)
                mm.then_inc(s_wov, 1)

            def start():
                adj_h(0, 0, 0)
                adj_h(0, 0, 1)
                adj_h(0, 0, 2)
                adj_h(0, 0, 3)
                q_row(0, 0)
                wov_block(0)
                v_to_row(0, 0)
                wov_block(1)
                attend(-1, 0, 0, 0, False)
                wov_block(2)
                attend(-1, 0, 0, 1, False)
                total(0, 0)
                rz_to_row(0, 0)
                adj_h(0, 1, 0)
                adj_h(0, 1, 1)
                wov_block(3)
                adj_h(0, 1, 2)
                adj_h(0, 1, 3)
                q_row(0, 1)
                v_to_row(0, 1)
                attend(-1, 0, 1, 0, False)
                attend(-1, 0, 1, 1, False)
                total(0, 1)
                rz_to_row(0, 1)
                pe.wait_ge(s_wlo, 2)

            def step(i, late, l0, ahead):
                p = i + 1
                if late:
                    rows_of(i - 1, 0)
                if l0:
                    adj_h(p, 0, 0)
                h2_transpose(i, 0)
                if l0:
                    adj_h(p, 0, 1)
                if late:
                    rows_of(i - 1, 1)
                h2_transpose(i, 1)
                if l0:
                    adj_h(p, 0, 2)
                h2_transpose(i, 2)
                h2_transpose(i, 3)
                if l0:
                    adj_h(p, 0, 3)
                z_lang(i, 0)
                if l0:
                    q_row(p, 0)
                z_lang(i, 1)
                z_lang(i, 2)
                if late:
                    k_transpose(i - 1, 0)
                if l0:
                    v_to_row(p, 0)
                z_lang(i, 3)
                if late:
                    mix(i - 1, 0, 4 * i + 4, l0)
                v_block(i, 0, late)
                if l0:
                    attend(i, p, 0, 0, late)
                if late:
                    k_transpose(i - 1, 1)
                if l0:
                    attend(i, p, 0, 1, late)
                    total(p, 0)
                v_block(i, 1, late)
                if l0:
                    rz_to_row(p, 0)
                    adj_h(p, 1, 0)
                v_block(i, 2, late)
                if l0:
                    adj_h(p, 1, 1)
                    adj_h(p, 1, 2)
                    adj_h(p, 1, 3)
                if late:
                    mix(i - 1, 1, 4 * p + 2 if l0 else 4 * PAIRS, l0)
                if l0:
                    q_row(p, 1)
                gram_lang(i, 0)
                gram_lang(i, 1)
                if l0:
                    v_to_row(p, 1)
                z_grav(i, 0)
                z_grav(i, 1)
                z_grav(i, 2)
                if l0:
                    attend(i, p, 1, 0, late)
                    attend(i, p, 1, 1, late)
                    total(p, 1)
                z_grav(i, 3)
                if l0:
                    rz_to_row(p, 1)
                v_block(i, 3, late)
                gram_grav(i, 0)
                gram_grav(i, 1)

            def finish():
                rows_of(PAIRS - 1, 0)
                rows_of(PAIRS - 1, 1)
                k_transpose(PAIRS - 1, 0)
                mix(PAIRS - 1, 0, 4 * PAIRS, False)
                k_transpose(PAIRS - 1, 1)
                mix(PAIRS - 1, 1, 4 * PAIRS, False)

            pe.wait_ge(s_ident, 2)
            pe.wait_ge(s_half, 2)
            pe.wait_ge(s_ae, 2)
            run(pe, start, step, finish)

        @block.vector
        def _(dve):
            def minus_hi(o, f, hi):
                return dve.tensor_tensor(o, f, hi.bitcast(fp32), ALU.subtract)

            def stats(layer, src, p, b):
                n, j = 2 * p + b, 2 * layer + b
                if layer == 0:
                    dve.wait_ge(s_xin[b], 16 * p + 16)
                    if not isinstance(p, int) or p > 0:
                        dve.wait_ge(s_h, 2 * p + b - 1)
                else:
                    dve.wait_ge(s_x1, n + 1)
                    dve.wait_ge(s_h2, 2 * p)
                for t in range(CB):
                    dve.bn_stats(bn[:, j, t], src[:, b, t]).then_inc(s_bn[layer], 1)
                dve.wait_ge(s_bn[layer], 2 * n + 2)
                dve.tensor_tensor(mv[:, j, 0], bn[:, j, :, 1], bn[:, j, :, 4], ALU.add)
                dve.tensor_tensor(mv[:, j, 1], bn[:, j, :, 1], bn[:, j, :, 4], ALU.subtract)
                dve.tensor_tensor(mv[:, j, 2], bn[:, j, :, 2], bn[:, j, :, 5], ALU.add).then_inc(s_mv[layer], 1)
                dve.wait_ge(s_mv[layer], 2 * n + 1)
                dve.tensor_scalar(nmean[:, j], mv[:, j, 0], -0.5, None, ALU.mult)
                dve.scalar_tensor_tensor(out=mv[:, j, 3], in0=mv[:, j, 1], scalar=0.25, in1=mv[:, j, 1],
                                         op0=ALU.mult, op1=ALU.mult)
                dve.tensor_scalar(mv[:, j, 4], mv[:, j, 2], 1.0 / N, LN_EPS, ALU.mult, ALU.add
                                  ).then_inc(s_mv[layer], 1)
                dve.wait_ge(s_mv[layer], 2 * n + 2)
                dve.tensor_tensor(var[:, j], mv[:, j, 3], mv[:, j, 4], ALU.add).then_inc(s_var[layer], 1)

            def ha_take(p, b, j):
                n = 8 * p + 4 * b + j + 1
                dve.wait_ge(s_ha, n)
                if j >= 2:
                    dve.wait_ge(s_halo, n - 2)
                dve.tensor_copy(qk[:, b, j], L0_BANK[j % 2][:, C:CE]).then_inc(s_qk, 1)
                dve.tensor_tensor(hab[:, j % 2], L0_BANK[j % 2][:, 0:C], bm_rows[:], ALU.add).then_inc(s_hab, 1)

            def ha_low(p, b, j):
                dve.wait_ge(s_hahi, 8 * p + 4 * b + j + 1)
                minus_hi(ha_lo[:, j], hab[:, j % 2], ha_hi[:, j]).then_inc(s_halo, 1)

            def q_tops(p, b):
                dve.wait_ge(s_qk, 8 * p + 4 * b + 4)
                dve.tensor_reduce(q_top[:, b:b + 1], qk[:, b, :, 0], AX.X, ALU.max).then_inc(s_qtop, 1)

            def arguments(p, b):
                n = 2 * p + b + 1
                dve.wait_ge(s_qt, n)
                dve.tensor_reduce(q_max[:, b:b + 1], L0_BANK[0][:, 0:128], AX.X, ALU.max).then_inc(s_qmax, 1)
                dve.wait_ge(s_qmax, n)
                dve.tensor_scalar(q_less[:, b], qk[:, b, :, 0], q_max[:, b:b + 1], None, ALU.subtract)
                dve.tensor_scalar(k_pos[:, b], qk[:, b, :, 1], q_max[:, b:b + 1], 0.0, ALU.add, ALU.max
                                  ).then_inc(s_arg, 1)

            def h_low(p, b):
                dve.wait_ge(s_hhi, 4 * p + 2 * b + 2)
                dve.wait_ge(s_ha, 8 * p + 4 * b)
                minus_hi(h_lo[:, 1], h[:, 1], h_hi[:, 1]).then_inc(s_hlo[1], 1)

            def p_make(p, b, j):
                if j == 0:
                    dve.wait_ge(s_vrow, 2 * p + b + 1)
                    dve.wait_ge(s_phi, 8 * p + 4 * b)
                    dve.wait_ge(s_plo, 8 * p + 4 * b)
                    dve.wait_ge(s_part, 6 * p + 3 * b)
                dve.tensor_scalar(p_f[:, j], v_row[:], col_b[:, b, j:j + 1], col_a[:, b, j:j + 1],
                                  ALU.mult, ALU.max).then_inc(s_pf, 1)

            def p_low(p, b, j):
                dve.wait_ge(s_num, 4 * p + 2 * b)
                dve.wait_ge(s_phi, 8 * p + 4 * b + j + 1)
                minus_hi(p_lo[:, j], p_f[:, j], p_hi[:, j]).then_inc(s_plo, 1)

            def z_column(p, b):
                dve.wait_ge(s_tt, 2 * p + b + 1)
                dve.reciprocal(z_inv[:, b], L0_BANK[0][:, 0:2 * NB].rearrange("p (j a) -> p j a", a=2)[:, :, 0]
                               ).then_inc(s_zinv, 1)

            def relu_over_z(p, b, o, kept):
                n = 2 * p + b
                dve.wait_ge(s_rz, n + 1)
                if kept:
                    dve.wait_ge(s_keep, n - 1)
                dve.wait_ge(s_num, 2 * n + o + 1)
                dve.scalar_tensor_tensor(out=x1[:, b, o], in0=SUM_BANK[o][:], scalar=0.0, in1=rz_row[:],
                                         op0=ALU.max, op1=ALU.mult).then_inc(s_y, 1)

            def residual(p, b):
                n = 2 * p + b
                dve.wait_ge(s_y, 2 * n + 2)
                dve.tensor_tensor(x1[:, b], x1[:, b], x_in[:, b], ALU.add).then_inc(s_x1, 1)

            def ht_low(i, f):
                dve.wait_ge(s_hthi, 4 * i + f + 1)
                m = slice(f * 128, (f + 1) * 128)
                minus_hi(ht_lo[:, :, m], HT_BANK[f][:].rearrange("p (t n) -> p t n", t=NB),
                         ht_hi[:, :, m]).then_inc(s_htlo, 1)

            def z_low(i, kind, e, psum):
                dve.wait_ge(s_zhi, 8 * i + 4 * kind + e + 1)
                minus_hi(z_lo[:, e], psum[:], z_hi[:, e]).then_inc(s_zlo, 1)

            def v_low(i, f):
                dve.wait_ge(s_vhi, 4 * i + f + 1)
                minus_hi(v_lo[:, f], V_BANK[f][:], v_hi[:, f]).then_inc(s_vlo, 1)

            def diagonal(i, b, g, s_copied, sq, s_sq, first):
                dve.wait_ge(s_copied, 2 * i + b + 1)
                for t in range(CB):
                    n = 4 * i + 2 * b + t
                    dve.wait_ge(s_sq, n)
                    if first is not None and b == 0 and t == 0:
                        dve.wait_ge(*first)
                    dve.scalar_tensor_tensor(out=junk[:], in0=g[:, b, t, t * 128:(t + 1) * 128], scalar=1.0,
                                             in1=ident[:], op0=ALU.mult, op1=ALU.mult,
                                             accum_out=sq[:, b, t:t + 1]).then_inc(s_sq, 1)

            def guard(i, b):
                dve.wait_ge(s_sql, 4 * i + 2 * b + 2)
                dve.tensor_scalar(sq_lm[:, b], sq_l[:, b], TINY * TINY, None, ALU.max).then_inc(s_sqlm, 1)

            def kernels_raw(i, b):
                dve.wait_ge(s_mrn, 2 * i + b + 1)
                for t in range(CB):
                    dve.scalar_tensor_tensor(out=k_f[:, b, t], in0=g_l[:, b, t], scalar=0.0, in1=k_f[:, b, t],
                                             op0=ALU.max, op1=ALU.mult,
                                             accum_out=deg[:, b, 0, t:t + 1]).then_inc(s_kl, 1)

            def distances(i, b):
                dve.wait_ge(s_rows, 2 * i + b + 1)
                dve.wait_ge(s_sqg, 4 * i + 2 * b + 2)
                for t in range(CB):
                    last = dve.scalar_tensor_tensor(out=g_g[:, b, t], in0=g_g[:, b, t], scalar=-2.0,
                                                    in1=rows[:, b, 1], op0=ALU.mult, op1=ALU.add)
                last.then_inc(s_dist, 1)
                dve.tensor_scalar(c_sq[:, b], sq_g[:, b], sig[:, 4:5], None, ALU.mult).then_inc(s_csq, 1)

            def kernels_masked(i, b):
                n = 4 * i + 2 * b
                for t in range(CB):
                    dve.wait_ge(s_exp, n + t + 1)
                    dve.scalar_tensor_tensor(out=g_g[:, b, t], in0=g_g[:, b, t], scalar=1.0, in1=adjz[:, t],
                                             op0=ALU.min, op1=ALU.mult,
                                             accum_out=deg[:, b, 1, t:t + 1]).then_inc(s_kg, 1)

            def coefficients(i, b):
                n = 4 * i + 2 * b
                dve.wait_ge(s_kl, n + 2)
                dve.wait_ge(s_kg, n + 2)
                dve.tensor_tensor(deg2[:, b, 0], deg[:, b, 0], r_norm[:, b], ALU.mult)
                dve.tensor_copy(deg2[:, b, 1], deg[:, b, 1]).then_inc(s_deg, 1)
                dve.wait_ge(s_deg, 6 * i + 3 * b + 1)
                dve.tensor_scalar(deg3[:, b], deg2[:, b], TINY, None, ALU.max).then_inc(s_deg, 1)
                dve.wait_ge(s_deg, 6 * i + 3 * b + 2)
                dve.reciprocal(deg_inv[:, b], deg3[:, b]).then_inc(s_deg, 1)
                dve.wait_ge(s_deg, 6 * i + 3 * b + 3)
                dve.scalar_tensor_tensor(out=coef[:, b, 0], in0=deg_inv[:, b, 0], scalar=gate[:, 3:4],
                                         in1=r_norm[:, b], op0=ALU.mult, op1=ALU.mult)
                dve.tensor_scalar(coef[:, b, 1], deg_inv[:, b, 1], gate[:, 4:5], None, ALU.mult
                                  ).then_inc(s_coef, 1)

            def k_sum(i, b):
                n = 4 * i + 2 * b
                for t in range(CB):
                    dve.wait_ge(s_ks, n + t + 1)
                    dve.scalar_tensor_tensor(out=k_f[:, b, t], in0=g_g[:, b, t], scalar=coef[:, b, 1, t:t + 1],
                                             in1=k_f[:, b, t], op0=ALU.mult, op1=ALU.add).then_inc(s_k, 1)

            def kt_low(i, b):
                dve.wait_ge(s_kthi, 2 * i + b + 1)
                minus_hi(kt_lo[:, b].rearrange("p t n -> p (t n)"), KT_BANK[b][:],
                         kt_hi[:, b].rearrange("p t n -> p (t n)")).then_inc(s_ktlo, 1)

            def output(i, b):
                dve.wait_ge(s_keep, 2 * i + b + 1)
                for t in range(CB):
                    dve.wait_ge(s_kv, 4 * i + 2 * b + t + 1)
                    dve.tensor_tensor(keep[:, b, t], SUM_BANK[t][:], keep[:, b, t], ALU.add).then_inc(s_out, 1)

            def weight_low(k):
                dve.wait_ge(s_chi, k + 1)
                minus_hi((z_lo, v_lo)[k][:], (keep, x1)[k][:].rearrange("p b t n -> p (b t) n"),
                         (z_hi, v_hi)[k][:]).then_inc(s_clo, 1)

            def wov_low(d):
                dve.wait_ge(s_ovhi, d + 1)
                minus_hi(wov_lo[:, d], L1_BANK[d][:], wov_hi[:, d]).then_inc(s_ovlo, 1)

            def start():
                h_low(0, 0)
                weight_low(0)
                ha_take(0, 0, 0)
                weight_low(1)
                ha_take(0, 0, 1)
                ha_low(0, 0, 0)
                ha_low(0, 0, 1)
                ha_take(0, 0, 2)
                ha_take(0, 0, 3)
                ha_low(0, 0, 2)
                q_tops(0, 0)
                dve.wait_ge(s_wlo, 1)
                arguments(0, 0)
                stats(0, x_in, 0, 1)
                p_make(0, 0, 0)
                p_make(0, 0, 1)
                p_make(0, 0, 2)
                p_low(0, 0, 0)
                p_low(0, 0, 1)
                p_low(0, 0, 2)
                p_make(0, 0, 3)
                ha_low(0, 0, 3)
                p_low(0, 0, 3)
                z_column(0, 0)
                wov_low(0)
                h_low(0, 1)
                ha_take(0, 1, 0)
                relu_over_z(0, 0, 0, False)
                relu_over_z(0, 0, 1, False)
                ha_take(0, 1, 1)
                wov_low(1)
                wov_low(2)
                ha_low(0, 1, 0)
                wov_low(3)
                ha_take(0, 1, 2)
                ha_low(0, 1, 1)
                residual(0, 0)
                ha_low(0, 1, 2)
                ha_take(0, 1, 3)
                q_tops(0, 1)
                arguments(0, 1)
                stats(0, x_in, 1, 0)
                p_make(0, 1, 0)
                p_make(0, 1, 1)
                p_make(0, 1, 2)
                stats(1, x1, 0, 0)
                p_low(0, 1, 0)
                ha_low(0, 1, 3)
                p_low(0, 1, 1)
                p_make(0, 1, 3)
                p_low(0, 1, 2)
                p_low(0, 1, 3)
                z_column(0, 1)
                relu_over_z(0, 1, 0, False)
                relu_over_z(0, 1, 1, False)
                h_low(1, 0)
                residual(0, 1)
                stats(1, x1, 0, 1)

            def step(i, late, l0, ahead):
                p = i + 1
                if l0:
                    ha_take(p, 0, 0)
                    ha_take(p, 0, 1)
                ht_low(i, 0)
                if l0:
                    ha_low(p, 0, 0)
                ht_low(i, 1)
                ht_low(i, 2)
                ht_low(i, 3)
                if l0:
                    ha_low(p, 0, 1)
                    ha_take(p, 0, 2)
                if late:
                    distances(i - 1, 0)
                if l0:
                    ha_take(p, 0, 3)
                    q_tops(p, 0)
                    ha_low(p, 0, 2)
                if late:
                    kernels_raw(i - 1, 0)
                if l0:
                    arguments(p, 0)
                if late:
                    kernels_masked(i - 1, 0)
                z_low(i, 0, 0, ZL_BANK[0])
                if late:
                    coefficients(i - 1, 0)
                if l0:
                    ha_low(p, 0, 3)
                if late:
                    k_sum(i - 1, 0)
                z_low(i, 0, 1, ZL_BANK[1])
                if late:
                    distances(i - 1, 1)
                z_low(i, 0, 2, ZL_BANK[2])
                if late:
                    kt_low(i - 1, 0)
                if l0:
                    p_make(p, 0, 0)
                if late:
                    kernels_raw(i - 1, 1)
                if l0:
                    p_make(p, 0, 1)
                    p_make(p, 0, 2)
                if late:
                    kernels_masked(i - 1, 1)
                if l0:
                    p_low(p, 0, 0)
                if late:
                    coefficients(i - 1, 1)
                    output(i - 1, 0)
                if l0:
                    p_make(p, 0, 3)
                    p_low(p, 0, 1)
                    p_low(p, 0, 2)
                    p_low(p, 0, 3)
                if late:
                    k_sum(i - 1, 1)
                if l0:
                    stats(0, x_in, p, 1)
                if late:
                    kt_low(i - 1, 1)
                if l0:
                    z_column(p, 0)
                    h_low(p, 1)
                z_low(i, 0, 3, ZL_BANK[3])
                if l0:
                    ha_take(p, 1, 0)
                v_low(i, 0)
                if l0:
                    ha_low(p, 1, 0)
                    relu_over_z(p, 0, 0, True)
                    ha_take(p, 1, 1)
                    relu_over_z(p, 0, 1, True)
                    ha_take(p, 1, 2)
                    ha_low(p, 1, 1)
                    ha_take(p, 1, 3)
                    ha_low(p, 1, 2)
                    q_tops(p, 1)
                v_low(i, 1)
                if l0:
                    arguments(p, 1)
                    residual(p, 0)
                if late:
                    output(i - 1, 1)
                v_low(i, 2)
                diagonal(i, 0, g_l, s_glc, sq_l, s_sql, (s_sqg, 4 * i))
                if l0:
                    stats(1, x1, p, 0)
                guard(i, 0)
                if l0:
                    p_make(p, 1, 0)
                diagonal(i, 1, g_l, s_glc, sq_l, s_sql, None)
                if l0:
                    p_make(p, 1, 1)
                    p_low(p, 1, 0)
                    p_make(p, 1, 2)
                    p_low(p, 1, 1)
                    p_low(p, 1, 2)
                    p_make(p, 1, 3)
                if ahead:
                    stats(0, x_in, p + 1, 0)
                guard(i, 1)
                if l0:
                    ha_low(p, 1, 3)
                    p_low(p, 1, 3)
                z_low(i, 1, 0, ZG_BANK[0])
                z_low(i, 1, 1, ZG_BANK[1])
                z_low(i, 1, 2, ZG_BANK[2])
                if ahead:
                    h_low(p + 1, 0)
                if l0:
                    z_column(p, 1)
                z_low(i, 1, 3, ZG_BANK[3])
                if l0:
                    relu_over_z(p, 1, 0, True)
                    relu_over_z(p, 1, 1, True)
                    residual(p, 1)
                    stats(1, x1, p, 1)
                diagonal(i, 0, g_g, s_ggc, sq_g, s_sqg, (s_sql, 4 * i + 4))
                v_low(i, 3)
                diagonal(i, 1, g_g, s_ggc, sq_g, s_sqg, None)

            def finish():
                distances(PAIRS - 1, 0)
                distances(PAIRS - 1, 1)
                kernels_masked(PAIRS - 1, 0)
                kernels_raw(PAIRS - 1, 0)
                kernels_raw(PAIRS - 1, 1)
                coefficients(PAIRS - 1, 0)
                kernels_masked(PAIRS - 1, 1)
                k_sum(PAIRS - 1, 0)
                coefficients(PAIRS - 1, 1)
                kt_low(PAIRS - 1, 0)
                k_sum(PAIRS - 1, 1)
                output(PAIRS - 1, 0)
                kt_low(PAIRS - 1, 1)
                output(PAIRS - 1, 1)

            stats(0, x_in, 0, 0)
            dve.wait_ge(s_ae, 1)
            minus_hi(ae_lo[:], ae_f, ae_hi[:]).then_inc(s_ae, 1)
            dve.wait_ge(s_gate_act, 2)
            dve.tensor_scalar(gate[:, 2:3], gate[:, 1:2], 1.0, None, ALU.add).then_inc(s_gate, 1)
            dve.tensor_scalar(sig[:, 2:3], sig[:, 1:2], sig[:, 1:2], 2.0, ALU.mult, ALU.mult).then_inc(s_gate, 1)
            dve.wait_ge(s_gate, 2)
            dve.reciprocal(gate[:, 3:4], gate[:, 2:3]).then_inc(s_gate, 1)
            dve.reciprocal(sig[:, 3:4], sig[:, 2:3]).then_inc(s_gate, 1)
            dve.wait_ge(s_gate, 4)
            dve.tensor_scalar(gate[:, 4:5], gate[:, 3:4], -1.0, 1.0, ALU.mult, ALU.add).then_inc(s_gate, 1)
            dve.tensor_scalar(sig[:, 4:5], sig[:, 3:4], -1.0, None, ALU.mult).then_inc(s_gate, 1)
            dve.wait_ge(s_gate, 6)
            dve.wait_ge(s_adjz, 1)
            dve.tensor_copy(gate[:, 5:6], gate[:, 4:5]).then_inc(s_gate, 1)
            run(dve, start, step, finish)


def kernel(x, adj, L0_gnn_wq, L0_gnn_wk, L0_gnn_bm, L1_gnn_W_lang, L1_gnn_W_grav, L1_gnn_W_V, L1_gnn_W_O,
           L1_gnn_gate_logit, L1_gnn_log_sigma):
    import numpy as np
    import concourse.bacc as bacc
    from concourse.bass_utils import run_bass_kernel_spmd

    arrays = {
        "x": np.ascontiguousarray(x),
        "adj": np.ascontiguousarray(adj),
        "adj_ext": np.concatenate([np.asarray(adj).T, np.asarray(L0_gnn_wq)[:, None],
                                   np.asarray(L0_gnn_wk)[:, None]], axis=1),
        "bm": np.ascontiguousarray(L0_gnn_bm),
        "w_lang_t": np.ascontiguousarray(np.asarray(L1_gnn_W_lang).T),
        "w_grav_t": np.ascontiguousarray(np.asarray(L1_gnn_W_grav).T),
        "w_v": np.ascontiguousarray(L1_gnn_W_V),
        "w_o_t": np.ascontiguousarray(np.asarray(L1_gnn_W_O).T),
        "gate_logit": np.ascontiguousarray(L1_gnn_gate_logit).reshape(1, 1),
        "log_sigma": np.ascontiguousarray(L1_gnn_log_sigma).reshape(1, 1),
    }
    nc = bacc.Bacc("TRN2", target_bir_lowering=False, num_devices=1, dynamic_dma_scratch_size=1024)
    args = [nc.dram_tensor(f"{n}_dram", a.shape, mybir.dt.from_np(a.dtype), kind="ExternalInput").ap()
            for n, a in arrays.items()]
    out = nc.dram_tensor("out_dram", x.shape, mybir.dt.from_np(np.dtype("float32")), kind="ExternalOutput").ap()
    adjacency_two_layer_kernel(nc, *args, out)
    r = run_bass_kernel_spmd(nc, [{f"{n}_dram": a for n, a in arrays.items()}], core_ids=[0])
    return r.results[0]["out_dram"]
```
